# Optimizing a Trainium2 kernel written in Bass

```python
import numpy as np
import jax
import jax.numpy as jnp

def _softmax(x, axis=-1):
    return jax.nn.softmax(x, axis=axis)

def _gelu(x):
    return jax.nn.gelu(x, approximate=True)

def _silu(x):
    return jax.nn.silu(x)

def _sigmoid(x):
    return jax.nn.sigmoid(x)

def _layernorm(x, axis=-1, eps=1e-05):
    m = jnp.mean(x, axis=axis, keepdims=True)
    v = jnp.var(x, axis=axis, keepdims=True)
    return (x - m) / jnp.sqrt(v + eps)

def _scatter_add(tgt, idx, src, axis=0):
    return tgt.at[idx].add(src)

def _segment_sum(src, seg, n):
    return jax.ops.segment_sum(src, seg, n)
kernel_name = 'mk_decoder_preln_d1_seqx_r4_b736e5'

def setup_inputs(seed: int=0):
    np.random.seed(seed)
    _w = jnp.asarray

    def _rec_inputs():
        import jax
        import jax.numpy as jnp
        _rk = jax.random.key(seed)
        x = -0.0002928 + 1 * jax.random.normal(jax.random.fold_in(_rk, 1), (16, 128, 256), jnp.float32)
        _lenS = 128 - jax.random.randint(jax.random.fold_in(_rk, 7), (16,), 0, max(1, 128 // 4) + 1, jnp.int32)
        _lenS2 = 128 - jax.random.randint(jax.random.fold_in(_rk, 8), (16,), 0, max(1, 128 // 4) + 1, jnp.int32)
        _ctx_1024P = jax.random.normal(jax.random.fold_in(_rk, 11), (16, 16, 256), jnp.float32)
        _ctx_1024c = jax.random.dirichlet(jax.random.fold_in(_rk, 511), 0.3 * jnp.ones((16,), jnp.float32), (16, 128))
        _ctx_1024t = jnp.einsum('bsk,bkd->bsd', _ctx_1024c, _ctx_1024P)
        _ctx_1024t = _ctx_1024t * jax.lax.rsqrt(jnp.mean(jnp.square(_ctx_1024t)) + 1e-12) * 0.953939
        ctx_1024 = -1.39393e-06 + 0.999914 * (_ctx_1024t + 0.3 * jax.random.normal(jax.random.fold_in(_rk, 611), (16, 128, 256), jnp.float32))
        return (x, ctx_1024)
    x, ctx_1024 = _rec_inputs()

    def _L0_attn_setup():
        import jax, jax.numpy as jnp
        import numpy as np
        import math
        D_MODEL = 256
        NUM_HEADS = 16
        D_HEAD = D_MODEL // NUM_HEADS
        BATCH = 4
        SEQ = 512

        def _trunc_normal(key, shape, sd):
            return sd * jax.random.truncated_normal(key, -3.0, 3.0, shape, dtype=jnp.float32)
        key = jax.random.key(seed)
        kx, kq, kk, kv, ko = jax.random.split(key, 5)
        sd = (2.0 / (NUM_HEADS * D_HEAD + D_MODEL)) ** 0.5
        x = jax.random.normal(kx, (BATCH, SEQ, D_MODEL), dtype=jnp.float32)
        WQ = _trunc_normal(kq, (NUM_HEADS, D_HEAD, D_MODEL), sd)
        WK = _trunc_normal(kk, (NUM_HEADS, D_HEAD, D_MODEL), sd)
        WV = _trunc_normal(kv, (NUM_HEADS, D_HEAD, D_MODEL), sd)
        WO = _trunc_normal(ko, (NUM_HEADS, D_MODEL, D_HEAD), sd)
        return {'x': x, 'WQ': WQ, 'WK': WK, 'WV': WV, 'WO': WO}
    _L0_attn_all = _L0_attn_setup()
    _L0_attn_in = {k: v for k, v in _L0_attn_all.items() if k in ('WQ', 'WK', 'WV', 'WO')}
    del _L0_attn_all

    def _L0_xattn_setup():
        import jax, jax.numpy as jnp
        import numpy as np
        D_MODEL = 256
        NUM_HEADS = 16
        D_K = D_MODEL // NUM_HEADS
        key = jax.random.key(seed)
        ks = jax.random.split(key, 11)
        B, S = (2, 512)
        scale = 1.0 / np.sqrt(D_MODEL)
        inp = {'Q': jax.random.normal(ks[0], (B, S, D_MODEL), jnp.float32), 'K': jax.random.normal(ks[1], (B, S, D_MODEL), jnp.float32), 'V': jax.random.normal(ks[2], (B, S, D_MODEL), jnp.float32), 'W_q': jax.random.normal(ks[3], (D_MODEL, D_MODEL), jnp.float32) * scale, 'b_q': jnp.zeros((D_MODEL,), jnp.float32), 'W_k': jax.random.normal(ks[4], (D_MODEL, D_MODEL), jnp.float32) * scale, 'b_k': jnp.zeros((D_MODEL,), jnp.float32), 'W_v': jax.random.normal(ks[5], (D_MODEL, D_MODEL), jnp.float32) * scale, 'b_v': jnp.zeros((D_MODEL,), jnp.float32), 'W_o': jax.random.normal(ks[6], (D_MODEL, D_MODEL), jnp.float32) * scale, 'b_o': jnp.zeros((D_MODEL,), jnp.float32)}
        return inp
    _L0_xattn_all = _L0_xattn_setup()
    _L0_xattn_in = {k: v for k, v in _L0_xattn_all.items() if k in ('W_q', 'b_q', 'W_k', 'b_k', 'W_v', 'b_v', 'W_o', 'b_o')}
    del _L0_xattn_all

    def _L0_ffn_setup():
        import jax, jax.numpy as jnp
        import numpy as np
        DIM = 256
        DEPTH = 2
        HEADS = 8
        DIM_HEAD = 64
        WINDOW = 128
        INNER = HEADS * DIM_HEAD
        HID = int(DIM * 4 * 2 / 3)
        B, N = (2, 2048)
        QK_SCALE = 8.0

        def shift_token(t):
            t1, t2 = jnp.split(t, 2, axis=-1)
            t2 = jnp.pad(t2, ((0, 0), (1, 0), (0, 0)))[:, :-1]
            return jnp.concatenate([t1, t2], axis=-1)

        def l2norm(t):
            return t / jnp.clip(jnp.linalg.norm(t, axis=-1, keepdims=True), 1e-12)

        def rotate_half(x):
            x1, x2 = jnp.split(x, 2, axis=-1)
            return jnp.concatenate([-x2, x1], axis=-1)

        def rotary_xpos(q, k):
            n = q.shape[-2]
            half_idx = jnp.arange(0, DIM_HEAD, 2, dtype=jnp.float32)
            inv_freq = 1.0 / 10000.0 ** (half_idx / DIM_HEAD)
            t = jnp.arange(n, dtype=jnp.float32)
            freqs = t[:, None] * inv_freq[None, :]
            freqs = jnp.concatenate([freqs, freqs], axis=-1)
            base = (half_idx + 0.4 * DIM_HEAD) / (1.4 * DIM_HEAD)
            power = (t - n // 2) / float(WINDOW // 2)
            scale = base[None, :] ** power[:, None]
            scale = jnp.concatenate([scale, scale], axis=-1)
            cos, sin = (jnp.cos(freqs), jnp.sin(freqs))
            q = q * cos * scale + rotate_half(q) * sin * scale
            k = k * cos / scale + rotate_half(k) * sin / scale
            return (q, k)

        def local_attention(q, k, v):
            b, h, n, d = q.shape
            w = n // WINDOW
            bq = q.reshape(b, h, w, WINDOW, d) * QK_SCALE
            bk = k.reshape(b, h, w, WINDOW, d)
            bv = v.reshape(b, h, w, WINDOW, d)

            def look_around(t):
                p = jnp.pad(t, ((0, 0), (0, 0), (1, 0), (0, 0), (0, 0)))
                return jnp.concatenate([p[:, :, :w], p[:, :, 1:]], axis=3)
            bk, bv = (look_around(bk), look_around(bv))
            bt = jnp.arange(n).reshape(w, WINDOW)
            btp = jnp.pad(bt, ((1, 0), (0, 0)), constant_values=-1)
            btk = jnp.concatenate([btp[:w], btp[1:]], axis=1)
            sim = jnp.einsum('bhwid,bhwjd->bhwij', bq, bk)
            i = bt[:, :, None]
            j = btk[:, None, :]
            mask = (i < j) | (i > j + WINDOW) | (j == -1)
            sim = jnp.where(mask, -jnp.finfo(sim.dtype).max, sim)
            attn = jax.nn.softmax(sim, axis=-1)
            out = jnp.einsum('bhwij,bhwjd->bhwid', attn, bv)
            return out.reshape(b, h, n, d)

        def _layer(x, wqkv, qs, ksc, wo, lg, lb, w1, b1, w2, b2):
            b, n, _ = x.shape
            h = shift_token(x)
            qkv = h @ wqkv
            q, k, v = jnp.split(qkv, 3, axis=-1)
            to_heads = lambda t: t.reshape(b, n, HEADS, DIM_HEAD).transpose(0, 2, 1, 3)
            q, k, v = (to_heads(q), to_heads(k), to_heads(v))
            q = l2norm(q) * qs
            k = l2norm(k) * ksc
            q, k = rotary_xpos(q, k)
            o = local_attention(q, k, v)
            o = o.transpose(0, 2, 1, 3).reshape(b, n, INNER)
            x = x + o @ wo
            h = shift_token(x)
            mu = h.mean(-1, keepdims=True)
            var = h.var(-1, keepdims=True)
            h = (h - mu) / jnp.sqrt(var + 1e-05) * lg + lb
            h = h @ w1 + b1
            a, g = jnp.split(h, 2, axis=-1)
            h = a * jax.nn.gelu(g, approximate=False)
            x = x + h @ w2 + b2
            return x
        key = jax.random.key(seed)
        ks = jax.random.split(key, 6)
        return {'x': jax.random.normal(ks[0], (B, N, DIM), jnp.float32), 'wqkv': jax.random.normal(ks[1], (DEPTH, DIM, 3 * INNER), jnp.float32) * 0.02, 'q_scale': jnp.ones((DEPTH, DIM_HEAD), jnp.float32), 'k_scale': jnp.ones((DEPTH, DIM_HEAD), jnp.float32), 'wo': jax.random.normal(ks[2], (DEPTH, INNER, DIM), jnp.float32) * 0.02, 'ln_g': jnp.ones((DEPTH, DIM), jnp.float32), 'ln_b': jnp.zeros((DEPTH, DIM), jnp.float32), 'w1': jax.random.normal(ks[3], (DEPTH, DIM, 2 * HID), jnp.float32) * 0.02, 'b1': jnp.zeros((DEPTH, 2 * HID), jnp.float32), 'w2': jax.random.normal(ks[4], (DEPTH, HID, DIM), jnp.float32) * 0.02, 'b2': jnp.zeros((DEPTH, DIM), jnp.float32)}
    _L0_ffn_all = _L0_ffn_setup()
    _L0_ffn_in = {k: v for k, v in _L0_ffn_all.items() if k in ('wqkv', 'q_scale', 'k_scale', 'wo', 'ln_g', 'ln_b', 'w1', 'b1', 'w2', 'b2')}
    del _L0_ffn_all
    return {'x': x, 'ctx_1024': ctx_1024, 'L0_attn_WQ': _L0_attn_in['WQ'], 'L0_attn_WK': _L0_attn_in['WK'], 'L0_attn_WV': _L0_attn_in['WV'], 'L0_attn_WO': _L0_attn_in['WO'], 'L0_xattn_W_q': _L0_xattn_in['W_q'], 'L0_xattn_b_q': _L0_xattn_in['b_q'], 'L0_xattn_W_k': _L0_xattn_in['W_k'], 'L0_xattn_b_k': _L0_xattn_in['b_k'], 'L0_xattn_W_v': _L0_xattn_in['W_v'], 'L0_xattn_b_v': _L0_xattn_in['b_v'], 'L0_xattn_W_o': _L0_xattn_in['W_o'], 'L0_xattn_b_o': _L0_xattn_in['b_o'], 'L0_ffn_wqkv': _L0_ffn_in['wqkv'], 'L0_ffn_q_scale': _L0_ffn_in['q_scale'], 'L0_ffn_k_scale': _L0_ffn_in['k_scale'], 'L0_ffn_wo': _L0_ffn_in['wo'], 'L0_ffn_ln_g': _L0_ffn_in['ln_g'], 'L0_ffn_ln_b': _L0_ffn_in['ln_b'], 'L0_ffn_w1': _L0_ffn_in['w1'], 'L0_ffn_b1': _L0_ffn_in['b1'], 'L0_ffn_w2': _L0_ffn_in['w2'], 'L0_ffn_b2': _L0_ffn_in['b2']}

def reference(x, ctx_1024, L0_attn_WQ, L0_attn_WK, L0_attn_WV, L0_attn_WO, L0_xattn_W_q, L0_xattn_b_q, L0_xattn_W_k, L0_xattn_b_k, L0_xattn_W_v, L0_xattn_b_v, L0_xattn_W_o, L0_xattn_b_o, L0_ffn_wqkv, L0_ffn_q_scale, L0_ffn_k_scale, L0_ffn_wo, L0_ffn_ln_g, L0_ffn_ln_b, L0_ffn_w1, L0_ffn_b1, L0_ffn_w2, L0_ffn_b2):
    import jax
    import jax.numpy as jnp

    def _L0_attn_ref(x, WQ, WK, WV, WO):
        import jax, jax.numpy as jnp
        import numpy as np
        import math
        D_MODEL = 256
        NUM_HEADS = 16
        D_HEAD = D_MODEL // NUM_HEADS
        BATCH = 4
        SEQ = 512

        def _trunc_normal(key, shape, sd):
            return sd * jax.random.truncated_normal(key, -3.0, 3.0, shape, dtype=jnp.float32)
        Q = jnp.einsum('bsd,hkd->bhsk', x, WQ)
        K = jnp.einsum('bsd,hkd->bhsk', x, WK)
        V = jnp.einsum('bsd,hkd->bhsk', x, WV)
        d_k = Q.shape[-1]
        scores = jnp.einsum('bhqd,bhkd->bhqk', Q, K) / math.sqrt(d_k)
        seq_len = x.shape[-2]
        causal = jnp.tril(jnp.ones((seq_len, seq_len), dtype=bool))
        scores = jnp.where(causal, scores, -jnp.inf)
        probs = jax.nn.softmax(scores, axis=-1)
        attn = jnp.einsum('bhqk,bhkv->bhqv', probs, V)
        return jnp.einsum('bhsv,hdv->bsd', attn, WO)

    def _L0_xattn_ref(Q, K, V, W_q, b_q, W_k, b_k, W_v, b_v, W_o, b_o):
        import jax, jax.numpy as jnp
        import numpy as np
        D_MODEL = 256
        NUM_HEADS = 16
        D_K = D_MODEL // NUM_HEADS
        B, S, _ = Q.shape
        H, d_k = (NUM_HEADS, D_K)
        q = Q @ W_q.T + b_q
        k = K @ W_k.T + b_k
        v = V @ W_v.T + b_v
        q = q.reshape(B, S, H, d_k).transpose(0, 2, 1, 3)
        k = k.reshape(B, S, H, d_k).transpose(0, 2, 1, 3)
        v = v.reshape(B, S, H, d_k).transpose(0, 2, 1, 3)
        scores = jnp.einsum('bhqd,bhkd->bhqk', q, k) / jnp.sqrt(jnp.float32(d_k)).astype(q.dtype)
        attn = jax.nn.softmax(scores, axis=-1)
        out = jnp.einsum('bhqk,bhkd->bhqd', attn, v)
        out = out.transpose(0, 2, 1, 3).reshape(B, S, H * d_k)
        return out @ W_o.T + b_o

    def _L0_ffn_ref(x, wqkv, q_scale, k_scale, wo, ln_g, ln_b, w1, b1, w2, b2):
        import jax, jax.numpy as jnp
        import numpy as np
        DIM = 256
        DEPTH = 2
        HEADS = 8
        DIM_HEAD = 64
        WINDOW = 128
        INNER = HEADS * DIM_HEAD
        HID = int(DIM * 4 * 2 / 3)
        B, N = (2, 2048)
        QK_SCALE = 8.0

        def shift_token(t):
            t1, t2 = jnp.split(t, 2, axis=-1)
            t2 = jnp.pad(t2, ((0, 0), (1, 0), (0, 0)))[:, :-1]
            return jnp.concatenate([t1, t2], axis=-1)

        def l2norm(t):
            return t / jnp.clip(jnp.linalg.norm(t, axis=-1, keepdims=True), 1e-12)

        def rotate_half(x):
            x1, x2 = jnp.split(x, 2, axis=-1)
            return jnp.concatenate([-x2, x1], axis=-1)

        def rotary_xpos(q, k):
            n = q.shape[-2]
            half_idx = jnp.arange(0, DIM_HEAD, 2, dtype=jnp.float32)
            inv_freq = 1.0 / 10000.0 ** (half_idx / DIM_HEAD)
            t = jnp.arange(n, dtype=jnp.float32)
            freqs = t[:, None] * inv_freq[None, :]
            freqs = jnp.concatenate([freqs, freqs], axis=-1)
            base = (half_idx + 0.4 * DIM_HEAD) / (1.4 * DIM_HEAD)
            power = (t - n // 2) / float(WINDOW // 2)
            scale = base[None, :] ** power[:, None]
            scale = jnp.concatenate([scale, scale], axis=-1)
            cos, sin = (jnp.cos(freqs), jnp.sin(freqs))
            q = q * cos * scale + rotate_half(q) * sin * scale
            k = k * cos / scale + rotate_half(k) * sin / scale
            return (q, k)

        def local_attention(q, k, v):
            b, h, n, d = q.shape
            w = n // WINDOW
            bq = q.reshape(b, h, w, WINDOW, d) * QK_SCALE
            bk = k.reshape(b, h, w, WINDOW, d)
            bv = v.reshape(b, h, w, WINDOW, d)

            def look_around(t):
                p = jnp.pad(t, ((0, 0), (0, 0), (1, 0), (0, 0), (0, 0)))
                return jnp.concatenate([p[:, :, :w], p[:, :, 1:]], axis=3)
            bk, bv = (look_around(bk), look_around(bv))
            bt = jnp.arange(n).reshape(w, WINDOW)
            btp = jnp.pad(bt, ((1, 0), (0, 0)), constant_values=-1)
            btk = jnp.concatenate([btp[:w], btp[1:]], axis=1)
            sim = jnp.einsum('bhwid,bhwjd->bhwij', bq, bk)
            i = bt[:, :, None]
            j = btk[:, None, :]
            mask = (i < j) | (i > j + WINDOW) | (j == -1)
            sim = jnp.where(mask, -jnp.finfo(sim.dtype).max, sim)
            attn = jax.nn.softmax(sim, axis=-1)
            out = jnp.einsum('bhwij,bhwjd->bhwid', attn, bv)
            return out.reshape(b, h, n, d)

        def _layer(x, wqkv, qs, ksc, wo, lg, lb, w1, b1, w2, b2):
            b, n, _ = x.shape
            h = shift_token(x)
            qkv = h @ wqkv
            q, k, v = jnp.split(qkv, 3, axis=-1)
            to_heads = lambda t: t.reshape(b, n, HEADS, DIM_HEAD).transpose(0, 2, 1, 3)
            q, k, v = (to_heads(q), to_heads(k), to_heads(v))
            q = l2norm(q) * qs
            k = l2norm(k) * ksc
            q, k = rotary_xpos(q, k)
            o = local_attention(q, k, v)
            o = o.transpose(0, 2, 1, 3).reshape(b, n, INNER)
            x = x + o @ wo
            h = shift_token(x)
            mu = h.mean(-1, keepdims=True)
            var = h.var(-1, keepdims=True)
            h = (h - mu) / jnp.sqrt(var + 1e-05) * lg + lb
            h = h @ w1 + b1
            a, g = jnp.split(h, 2, axis=-1)
            h = a * jax.nn.gelu(g, approximate=False)
            x = x + h @ w2 + b2
            return x
        for l in range(DEPTH):
            x = _layer(x, wqkv[l], q_scale[l], k_scale[l], wo[l], ln_g[l], ln_b[l], w1[l], b1[l], w2[l], b2[l])
        return x
    x = x + _L0_attn_ref(_layernorm(x, axis=-1), L0_attn_WQ, L0_attn_WK, L0_attn_WV, L0_attn_WO)
    x = x + _L0_xattn_ref(_layernorm(x, axis=-1), ctx_1024, ctx_1024, L0_xattn_W_q, L0_xattn_b_q, L0_xattn_W_k, L0_xattn_b_k, L0_xattn_W_v, L0_xattn_b_v, L0_xattn_W_o, L0_xattn_b_o)
    x = x + _L0_ffn_ref(_layernorm(x, axis=-1), L0_ffn_wqkv, L0_ffn_q_scale, L0_ffn_k_scale, L0_ffn_wo, L0_ffn_ln_g, L0_ffn_ln_b, L0_ffn_w1, L0_ffn_b1, L0_ffn_w2, L0_ffn_b2)
    return x

_drawn_inputs = setup_inputs


def setup_inputs(seed=0):
    import zlib

    import numpy as np

    out = dict(_drawn_inputs(seed))
    spreads = {'L0_xattn_b_q': (0.0, 0.406),
     'L0_xattn_b_k': (0.0, 0.8),
     'L0_xattn_b_v': (0.0, 0.1),
     'L0_xattn_b_o': (0.0, 0.1),
     'L0_ffn_q_scale': (1.0, 0.6),
     'L0_ffn_k_scale': (1.0, 0.6),
     'L0_ffn_ln_g': (1.0, 0.6),
     'L0_ffn_ln_b': (0.0, 0.8),
     'L0_ffn_b1': (0.0, 0.8),
     'L0_ffn_b2': (0.0, 0.1)}
    factors = {}
    for name, (base, spread) in spreads.items():
        noise = np.random.default_rng([zlib.crc32(name.encode()), seed]).standard_normal(out[name].shape)
        drawn = base * np.exp(spread * noise) if base else spread * noise
        out[name] = jnp.asarray(drawn.astype(out[name].dtype))
    for name, factor in factors.items():
        out[name] = (out[name] * factor).astype(out[name].dtype)
    return out
```

```python
from contextlib import ExitStack

import numpy as np

import concourse.bass as bass
from concourse import mybir

F32 = mybir.dt.float32
I32 = mybir.dt.int32
ALU = mybir.AluOpType
ACT = mybir.ActivationFunctionType
AX = mybir.AxisListType

P = 128
NS = 16
D = 256
KT = D // P
EPS = 1e-5
NORM_FLOOR = 1e-24
MASKED = -3.0e38
QUAD = 4
BANK = 512
DEPTH = 2
HEADS = 8
DH = 64
INNER = HEADS * DH
HID = int(D * 4 * 2 / 3)
FT = -(-HID // P)
TILES = [(i * P, min(P, HID - i * P)) for i in range(FT)]
RSQRT_MAGIC = float(0x5F3759DF)
RSQRT_MAGIC_OF_HALF = float(0x5F3759DF - 0x400000)
NEWTON = 3
RSQRT_OPS = 2 + 3 * NEWTON


def wait(eng, sem, count):
    if isinstance(count, int) and count <= 0:
        return
    eng.wait_ge(sem, count)


def fewest(a, b):
    return min(a, b) if isinstance(a, int) else a


def is_sample(n):
    return not isinstance(n, int) or 0 <= n < NS


AHEAD, BEHIND = 2, 3
LOOP_FROM = 4


def over_samples(eng, body):
    for s in range(-AHEAD, LOOP_FROM):
        body(s, s % 2)
    with eng.Fori(LOOP_FROM // 2, NS // 2 - 1) as pair:
        body(pair * 2, 0)
        body(pair * 2 + 1, 1)
    for s in range(NS - 2, NS + BEHIND):
        body(s, s % 2)


def rsqrt(dve, y, x, t, sem, base):
    dve.tensor_scalar(t.bitcast(I32), x.bitcast(I32), 1, None, ALU.logical_shift_right).then_inc(sem, 1)
    dve.wait_ge(sem, base + 1)
    dve.tensor_scalar(y.bitcast(I32), t.bitcast(I32), -1.0, RSQRT_MAGIC, ALU.mult, ALU.add).then_inc(sem, 1)
    for i in range(NEWTON):
        dve.wait_ge(sem, base + 2 + 3 * i)
        dve.scalar_tensor_tensor(t, y, -0.5, y, ALU.mult, ALU.mult).then_inc(sem, 1)
        dve.wait_ge(sem, base + 3 + 3 * i)
        dve.tensor_tensor(t, t, x, ALU.mult).then_inc(sem, 1)
        dve.wait_ge(sem, base + 4 + 3 * i)
        dve.scalar_tensor_tensor(y, t, 1.5, y, ALU.add, ALU.mult).then_inc(sem, 1)


def decoder_kernel(nc, a, out):
    with ExitStack() as ctx:
        def sb(name, shape, dt=F32):
            return ctx.enter_context(nc.sbuf_tensor(name, shape, dt))

        def sem(name):
            return ctx.enter_context(nc.semaphore(name))

        X = sb("X", [P, NS, D])
        Y = sb("Y", [P, NS, D])
        YS = sb("YS", [P, NS, P])
        bn = sb("bn", [P, 2, 6])
        mv = sb("mv", [P, NS, 2])
        vare = sb("vare", [P, NS])
        rstd = sb("rstd", [P, NS])
        nt = sb("nt", [P, NS])

        w_self = sb("w_self", [P, KT, 3 * D])
        wo_self = sb("wo_self", [P, KT, D])
        w_cross = sb("w_cross", [P, KT, 3 * D])
        wo_cross = sb("wo_cross", [P, KT, D])
        b_cross = sb("b_cross", [P, 4, D])
        w_qkv = sb("w_qkv", [P, KT, 3 * INNER])
        wo_loc = sb("wo_loc", [P, INNER // P, D])
        w_1 = sb("w_1", [P, KT, 2 * HID])
        w_2 = sb("w_2", [P, FT, D])
        b_1 = sb("b_1", [P, DEPTH, 2, FT])
        b_2 = sb("b_2", [P, DEPTH, D])
        ln_g = sb("ln_g", [P, DEPTH, KT])
        ln_b = sb("ln_b", [P, DEPTH, KT])
        qks = sb("qks", [P, DEPTH, 2, DH])
        ident = sb("ident", [P, P])
        shift = sb("shift", [P, P])
        mask = sb("mask", [P, P])
        rot = sb("rot", [P, 2, 2, DH])
        rots = sb("rots", [P, 2, 2, DH])

        xn = [sb(f"xn{i}", [P, D]) for i in range(2)]
        cx = [sb(f"cx{i}", [P, D]) for i in range(2)]
        xT = [sb(f"xT{i}", [P, 2 * KT, P]) for i in range(2)]
        qkb = [sb(f"qkb{i}", [P, 2, INNER]) for i in range(2)]
        qT = [sb(f"qT{i}", [P, 4, P]) for i in range(2)]
        kB = [sb(f"kB{i}", [P, 2, 8 * P]) for i in range(2)]
        own = sb("own", [P, 8])
        V = sb("V", [P, NS, INNER])
        masked = [sb(f"masked{i}", [P, QUAD, P]) for i in range(2)]
        probs = [sb(f"probs{i}", [P, QUAD, P]) for i in range(2)]
        pT = [sb(f"pT{i}", [P, QUAD, P]) for i in range(2)]
        negmax = [sb(f"negmax{i}", [P, QUAD]) for i in range(2)]
        rsum = [sb(f"rsum{i}", [P, 16]) for i in range(2)]
        row = [sb(f"row{i}", [P, D]) for i in range(2)]
        mv1 = sb("mv1", [P, 2])
        rec = sb("rec", [P, 16])
        ob = sb("ob", [P, INNER])
        oT = sb("oT", [P, INNER // P, P])
        three_halves = sb("three_halves", [P, 16])
        raw = sb("raw", [P, 2, INNER])
        sq = sb("sq", [P, 2, INNER])
        rot_ab = sb("rot_ab", [P, 4, INNER])
        ra, rb = rot_ab[:, 0:2, :], rot_ab[:, 2:4, :]
        ss = [sb(f"ss{i}", [P, 16]) for i in range(2)]
        rn = [sb(f"rn{i}", [P, 16]) for i in range(2)]
        rt = [sb(f"rt{i}", [P, 16]) for i in range(2)]
        GS = 2
        hn = sq[:, 0, :].rearrange("p (g d) -> p g d", g=GS)
        hT = sq[:, 1, :].rearrange("p (k n) -> p k n", k=KT)
        gate = [ob[:, i * GS * P:(i + 1) * GS * P] for i in range(2)]
        hid = rot_ab[:].rearrange("p a b -> p (a b)")[:, 0:FT * GS * P].rearrange("p (f n) -> p f n", f=FT)

        banks = [ctx.enter_context(nc.psum_tensor(f"bank{i}", [P, BANK], F32)) for i in range(8)]

        ld_x = [sem(f"ld_x{i}") for i in range(4)]
        ld_const = sem("ld_const")
        ld_self = sem("ld_self")
        ld_cross = sem("ld_cross")
        ld_loc = sem("ld_loc")
        ld_mlp = sem("ld_mlp")
        ld_small = sem("ld_small")
        n_loads = {}

        def load(eng, s, dst, src):
            eng.dma_start(dst, src).then_inc(s, 16)
            n_loads[s.name] = n_loads.get(s.name, 0) + 16

        def load_mlp(eng, s, l):
            full = HID // P * P
            load(eng, s, w_1[:], a["w_1"][l])
            load(eng, s, w_2[:, 0:HID // P, :], a["w_2"][l, 0:full, :].rearrange("(f p) d -> p f d", p=P))
            load(eng, s, w_2[0:HID - full, HID // P, :], a["w_2"][l, full:HID, :])

        x_t = a["x"].rearrange("s t d -> t s d")

        with nc.Block() as block:
            @block.sync
            def _(sp):
                for i in range(4):
                    sp.dma_start(X[:, 4 * i:4 * i + 4, :], x_t[:, 4 * i:4 * i + 4, :]).then_inc(ld_x[i], 16)
                    if i == 0:
                        load(sp, ld_const, ident[:], a["c_ident"])
                        load(sp, ld_self, w_self[:], a["w_self"])
                        load(sp, ld_const, mask[:], a["c_mask"])
                        load(sp, ld_self, wo_self[:], a["wo_self"])
                load(sp, ld_const, own[:], a["c_own"])
                load(sp, ld_const, shift[:], a["c_shift"])
                load(sp, ld_const, rot[:], a["c_rot"])
                load(sp, ld_cross, w_cross[:], a["w_cross"])
                load(sp, ld_cross, wo_cross[:], a["wo_cross"])
                for i, b in enumerate(("b_q", "b_k", "b_v", "b_o")):
                    load(sp, ld_cross, b_cross[:, i, :], a[b].broadcast_to([P, D]))
                load(sp, ld_loc, w_qkv[:], a["w_qkv"][0])
                load(sp, ld_loc, wo_loc[:], a["wo_loc"][0])
                load(sp, ld_small, b_1[:], a["b1"])
                load(sp, ld_small, ln_g[:], a["ln_g"])
                load(sp, ld_small, ln_b[:], a["ln_b"])
                for l in range(DEPTH):
                    load(sp, ld_small, qks[:, l, 0, :], a["q_scale"][l:l + 1, :].broadcast_to([P, DH]))
                    load(sp, ld_small, qks[:, l, 1, :], a["k_scale"][l:l + 1, :].broadcast_to([P, DH]))
                    load(sp, ld_small, b_2[:, l, :], a["b2"][l:l + 1, :].broadcast_to([P, D]))
                load_mlp(sp, ld_mlp, 0)

            stat = sem("stat")
            rs0 = sem("rs0")

            @block.vector
            def _(dve):
                done = 0
                for half, (lo, hi) in enumerate(((0, 4), (4, NS))):
                    for s in range(lo, hi):
                        if s % 4 == 0:
                            dve.wait_ge(ld_x[s // 4], 16)
                        wait(dve, stat, done)
                        dve.bn_stats(bn[:, 0, :], X[:, s, :]).then_inc(stat, 1)
                        dve.wait_ge(stat, done + 1)
                        dve.bn_aggr(mv[:, s, :], bn[:, 0, :]).then_inc(stat, 1)
                        done += 2
                    dve.wait_ge(stat, done)
                    dve.tensor_scalar(vare[:, lo:hi], mv[:, lo:hi, 1], EPS, None, ALU.add).then_inc(stat, 1)
                    done += 1
                    dve.wait_ge(stat, done)
                    rsqrt(dve, rstd[:, lo:hi], vare[:, lo:hi], nt[:, lo:hi], rs0, half * RSQRT_OPS)
                dve.wait_ge(rs0, 2 * RSQRT_OPS)

        m = Shared()
        m.three_halves, m.GS, m.V, m.X, m.Y, m.YS = three_halves, GS, V, X, Y, YS
        m.a, m.b_1, m.b_2, m.b_cross, m.banks, m.bn = a, b_1, b_2, b_cross, banks, bn
        m.cx, m.gate, m.hT, m.hid, m.hn, m.ident = cx, gate, hT, hid, hn, ident
        m.kB, m.ld_const, m.ld_cross, m.ld_loc, m.ld_mlp, m.ld_self = kB, ld_const, ld_cross, ld_loc, ld_mlp, ld_self
        m.ld_small, m.ln_b, m.ln_g, m.load_mlp, m.mask, m.masked = ld_small, ln_b, ln_g, load_mlp, mask, masked
        m.mv, m.mv1, m.n_loads, m.negmax, m.nt, m.oT = mv, mv1, n_loads, negmax, nt, oT
        m.ob, m.own, m.pT, m.probs, m.qT, m.qkb = ob, own, pT, probs, qT, qkb
        m.qks, m.ra, m.raw, m.rb, m.rec, m.rn = qks, ra, raw, rb, rec, rn
        m.rot, m.rots, m.row, m.rstd, m.rsum, m.rt = rot, rots, row, rstd, rsum, rt
        m.shift, m.sq, m.ss, m.vare, m.w_1, m.w_2 = shift, sq, ss, vare, w_1, w_2
        m.w_cross, m.w_qkv, m.w_self, m.wo_cross, m.wo_loc, m.wo_self = w_cross, w_qkv, w_self, wo_cross, wo_loc, wo_self
        m.xT, m.xn = xT, xn
        attention(nc, m, "self", 0)
        attention(nc, m, "cross", 0)
        for l in range(DEPTH):
            attention(nc, m, "local", l)
            mlp(nc, m, l, out)


class Shared:
    pass


def release(nc, signals):
    nc.clear_and_free_semaphores(list(signals.values()))
    nc.all_engine_barrier()


def attention(nc, m, kind, layer):
    a = m.a
    cross, local = kind == "cross", kind == "local"
    causal = not cross
    tag = f"{kind}{layer}_"
    heads, dh = (HEADS, DH) if local else (16, 16)
    per_tile = P // dh
    width = heads * dh
    NQ = heads // QUAD
    LAG = 2
    OUT = 2 if local else 1
    OT_TILES = width // P
    nT = 2 * KT if cross else KT

    PJ0, PJ1, TR0, TR1, S0, S1, PTB, OB = m.banks
    S = (S0, S1)
    WB = PJ1 if local else PJ0

    G = {n: nc.alloc_semaphore(name=tag + n) for n in (
        "xn_ready", "xT_bank", "xT_ready", "projA", "projB", "evacA", "evacB", "qT_bank", "kT_bank",
        "qT_ready", "kT_ready", "quad_scores", "quad_negmax", "quad_probs", "quad_pT_bank", "quad_pT",
        "quad_out", "rec_ready", "o_ready", "oT_bank", "oT_ready", "wo_bank", "added", "stats",
        "aggregated", "mv_kept", "kept", "start",
        *(["quad_masked"] if causal else []),
        *(["qk_ready", "ctx0", "ctx1", "biased"] if cross else []),
        *(["qk_ready", "projC", "evacC", "squared", "rotated", "sumsq", "clipped", "halved", "seeded", "newton", "rotsum",
           "shifted", "y_kept", "scaled", "y_ready", "half_shifted", "zeroed", "weights"] if local else []))}
    ctx_in = (G["ctx0"], G["ctx1"]) if cross else None
    KR = 2
    XR = 2 if local else 1
    ROT = 6
    qk_done = G["qk_ready"] if cross or local else G["evacA"]

    def key_blocks(par):
        return m.kB[par][:].rearrange("p a b -> p (a b)").rearrange("p (t c) -> p t c", t=OT_TILES)

    with nc.Block() as block:
        if cross:
            @block.sync
            def _(sp):
                def body(s, par):
                    if not is_sample(s):
                        return
                    wait(sp, G["xT_bank"], s - 1)
                    sp.dma_start(m.cx[par][:], a["ctx"][s]).then_inc(ctx_in[par], 16)
                over_samples(sp, body)
        if local and layer:
            @block.sync
            def _(sp):
                sp.dma_start(m.w_qkv[:], a["w_qkv"][layer]).then_inc(G["weights"], 16)
                sp.dma_start(m.wo_loc[:], a["wo_loc"][layer]).then_inc(G["weights"], 16)
                m.load_mlp(sp, m.ld_mlp, layer)

        @block.tensor
        def _(pe):
            w_in = m.w_qkv if local else m.w_cross if cross else m.w_self
            w_out = m.wo_loc if local else m.wo_cross if cross else m.wo_self

            def transpose_inputs(n, par):
                if not is_sample(n):
                    return
                pe.wait_ge(G["xn_ready"], n + 1)
                if cross:
                    pe.wait_ge(ctx_in[par], (n - par) * 8 + 16)
                wait(pe, G["xT_ready"], XR * n)
                wait(pe, G["qT_ready"], n - 1 if local else n)
                for i in range(nT):
                    src = m.xn[par] if i < KT else m.cx[par]
                    last = pe.transpose(TR0[:, i * P:(i + 1) * P], src[:, i % KT * P:(i % KT + 1) * P], m.ident[:])
                last.then_inc(G["xT_bank"], 1)

            def project(bank, par, lo, n_cols, signal, tiles=0):
                for k in range(KT):
                    last = pe.matmul(bank[:, 0:n_cols], m.xT[par][:, tiles + k, :],
                                     w_in[:, k, lo:lo + n_cols], start=k == 0, stop=k == KT - 1)
                last.then_inc(signal, 1)

            def project_a(n, par):
                if not is_sample(n):
                    return
                pe.wait_ge(G["xT_ready"], XR * (n + 1))
                if local:
                    wait(pe, G["evacC"], n)
                else:
                    wait(pe, G["evacA"], n)
                    wait(pe, G["added"], n - 3)
                project(PJ0, par, 0, D if cross else 2 * D, G["projA"])

            def project_b(n, par):
                if not is_sample(n):
                    return
                if not local:
                    wait(pe, G["evacB"], n)
                else:
                    wait(pe, G["evacB"], n)
                    wait(pe, G["added"], n - 4)
                    project(PJ1, par, INNER, INNER, G["projB"])
                    return
                if cross:
                    project(PJ1, par, D, 2 * D, G["projB"], KT)
                else:
                    project(PJ1, par, 2 * D, D, G["projB"])

            def project_c(n, par):
                if not local or not is_sample(n):
                    return
                pe.wait_ge(G["evacA"], n + 1)
                project(PJ0, par, 2 * INNER, INNER, G["projC"])

            def transpose_qk(n, par):
                if not is_sample(n):
                    return
                pe.wait_ge(qk_done, n + 1)
                wait(pe, G["xT_ready"], XR * (fewest(n + 2, NS) if local else n + 1))
                for i in range(OT_TILES):
                    last = pe.transpose(TR0[:, i * P:(i + 1) * P], m.qkb[par][:, 0, i * P:(i + 1) * P], m.ident[:])
                last.then_inc(G["qT_bank"], 1)
                wait(pe, G["kT_ready"], KR * n)
                wait(pe, G["oT_ready"], n - 2)
                if local:
                    wait(pe, G["kept"], n - 3)
                for i in range(OT_TILES):
                    last = pe.transpose(TR1[:, i * P:(i + 1) * P], m.qkb[par][:, 1, i * P:(i + 1) * P], m.ident[:])
                last.then_inc(G["kT_bank"], 1)

            def scores(s, par, q):
                if not is_sample(s):
                    return
                if q == 0:
                    pe.wait_ge(G["qT_ready"], s + 1)
                    pe.wait_ge(G["kT_ready"], KR * (s + 1))
                wait(pe, G["quad_masked"] if causal else G["quad_probs"], s * NQ + q - 1)
                t, n_heads = (2 * q, 2) if local else (q // 2, QUAD)
                for i in range(QUAD // n_heads):
                    at = 0 if local else q % 2 * QUAD * P
                    last = pe.matmul(S[q % 2][:, i * n_heads * P:(i + 1) * n_heads * P], m.qT[par][:, t + i, :],
                                     key_blocks(par)[:, t + i, at:at + n_heads * P], start=True, stop=True)
                last.then_inc(G["quad_scores"], 1)

            def transpose_probs(s, q):
                if not is_sample(s):
                    return
                pe.wait_ge(G["quad_probs"], s * NQ + q + 1)
                wait(pe, G["quad_pT"], s * NQ + q)
                for j in range(QUAD):
                    last = pe.transpose(PTB[:, j * P:(j + 1) * P], m.probs[q % 2][:, j, :], m.ident[:])
                last.then_inc(G["quad_pT_bank"], 1)

            def attend(s, q):
                if not is_sample(s):
                    return
                if q == 0:
                    pe.wait_ge(G["evacC"] if local else G["evacB"], s + 1)
                    wait(pe, G["o_ready"], s)
                pe.wait_ge(G["quad_pT"], s * NQ + q + 1)
                for j in range(QUAD):
                    h = QUAD * q + j
                    last = pe.matmul(OB[:, h * dh:(h + 1) * dh], m.pT[q % 2][:, j, :],
                                     m.V[:, s, h * dh:(h + 1) * dh], start=True, stop=True)
                last.then_inc(G["quad_out"], 1)

            def transpose_out(n):
                if not is_sample(n):
                    return
                pe.wait_ge(G["o_ready"], n + 1)
                wait(pe, G["kT_ready"], KR * fewest(n + 3, NS))
                if local:
                    wait(pe, G["kept"], n - 1)
                wait(pe, G["oT_ready"], n)
                for i in range(OT_TILES):
                    last = pe.transpose(TR1[:, i * P:(i + 1) * P], m.ob[:, i * P:(i + 1) * P], m.ident[:])
                last.then_inc(G["oT_bank"], 1)

            def project_out(n):
                if not is_sample(n):
                    return
                pe.wait_ge(G["oT_ready"], n + 1)
                wait(pe, G["evacB"] if local else G["evacA"], fewest(n + OUT + AHEAD + 1, NS))
                wait(pe, G["added"], n)
                for i in range(OT_TILES):
                    last = pe.matmul(WB[:, 0:D], m.oT[:, i, :], w_out[:, i, :],
                                     start=i == 0, stop=i == OT_TILES - 1)
                last.then_inc(G["wo_bank"], 1)

            def shift_tokens(n, par):
                if not local or not is_sample(n):
                    return
                pe.wait_ge(G["added"], n + 1)
                wait(pe, G["oT_ready"], fewest(n + 2, NS))
                pe.matmul(TR1[:, 0:P], m.shift[:], m.row[par][:, P:D], start=True, stop=True).then_inc(G["shifted"], 1)

            pe.wait_ge(m.ld_const, m.n_loads[m.ld_const.name])
            if local and layer:
                pe.wait_ge(G["weights"], 32)
            else:
                ld = m.ld_loc if local else m.ld_cross if cross else m.ld_self
                pe.wait_ge(ld, m.n_loads[ld.name])

            def body(s, par):
                nxt = s + AHEAD
                for q in range(NQ):
                    scores(s, par, q)
                    before = (s, q - LAG) if q >= LAG else (s - 1, NQ + q - LAG)
                    if local and q == 0:
                        transpose_inputs(nxt, par)
                    transpose_probs(*before)
                    if local and q == 0:
                        project_a(nxt, par)
                        transpose_out(s - 2)
                        project_b(nxt, par)
                        shift_tokens(s - 3, 1 - par)
                    elif local:
                        project_c(nxt, par)
                        transpose_qk(s + 1, 1 - par)
                        project_out(s - 2)
                    elif q == 0:
                        transpose_qk(s + 1, 1 - par)
                        transpose_inputs(nxt, par)
                    elif q == 1:
                        project_a(nxt, par)
                    elif q == 2:
                        project_b(nxt, par)
                        transpose_out(s - 1)
                    else:
                        project_out(s - 1)
                    attend(*before)

            over_samples(pe, body)

        @block.vector
        def _(dve):
            def normed(n, par):
                if not is_sample(n):
                    return
                wait(dve, G["xT_bank"], n - 1)
                if local and layer:
                    copy(m.xn[par][:], m.Y[:, n, :]).then_inc(G["xn_ready"], 1)
                    return
                dve.tensor_scalar(m.xn[par][:], m.X[:, n, :], m.mv[:, n, 0:1], m.rstd[:, bass.ds(n, 1)],
                                  ALU.subtract, ALU.mult).then_inc(G["xn_ready"], 1)
                if local:
                    dve.tensor_scalar(m.Y[:, n, :], m.X[:, n, :], m.mv[:, n, 0:1], m.rstd[:, bass.ds(n, 1)],
                                      ALU.subtract, ALU.mult).then_inc(G["y_ready"], 1)

            def copy(out, in_):
                return dve.tensor_scalar(out, in_, 1.0, None, ALU.mult)

            def heads_of(ap):
                return ap.rearrange("p (h c) -> p h c", h=heads)

            def read_a(n, par):
                if local or not is_sample(n):
                    return
                dve.wait_ge(G["projA"], n + 1)
                wait(dve, G["kT_bank"], n - 1)
                if cross:
                    dve.tensor_tensor(m.qkb[par][:, 0, 0:D], PJ0[:, 0:D], m.b_cross[:, 0, :], ALU.add).then_inc(G["evacA"], 1)
                else:
                    dve.tensor_copy(m.qkb[par][:, :, 0:D], PJ0[:].rearrange("p (w c) -> p w c", w=2)).then_inc(G["evacA"], 1)

            def read_b(n, par):
                if not is_sample(n):
                    return
                dve.wait_ge(G["projB"], n + 1)
                if cross:
                    dve.tensor_tensor(m.qkb[par][:, 1, 0:D], PJ1[:, 0:D], m.b_cross[:, 1, :], ALU.add).then_inc(G["qk_ready"], 1)
                    dve.tensor_tensor(m.V[:, n, 0:D], PJ1[:, D:2 * D], m.b_cross[:, 2, :], ALU.add).then_inc(G["evacB"], 1)
                else:
                    copy(m.V[:, n, 0:D], PJ1[:, 0:D]).then_inc(G["evacB"], 1)

            def rotate(n, which):
                if not is_sample(n):
                    return
                dve.wait_ge(G["evacB"] if which else G["evacA"], n + 1)
                wait(dve, G["rotsum"], n)

                def factor(kind, lo, hi):
                    return m.rots[:, which, kind, lo:hi].unsqueeze(1).broadcast_to([P, heads, hi - lo])

                x, ra, rb = (heads_of(ap[:, which, :]) for ap in (m.raw, m.ra, m.rb))
                dve.tensor_tensor(ra, x, factor(0, 0, dh), ALU.mult).then_inc(G["rotated"], 1)
                for lo, hi in ((0, dh // 2), (dh // 2, dh)):
                    dve.tensor_tensor(rb[:, :, lo:hi], x[:, :, dh // 2 - lo:dh - lo],
                                      factor(1, lo, hi), ALU.mult).then_inc(G["rotated"], 1)

            def norms(n, par):
                if not local or not is_sample(n):
                    return
                ss, rn, rt = m.ss[par], m.rn[par], m.rt[par]
                wait(dve, G["qk_ready"], n - 1)
                dve.wait_ge(G["squared"], 2 * n + 2)
                dve.tensor_reduce(ss[:], m.sq[:].rearrange("p w (h c) -> p (w h) c", h=heads), AX.X,
                                  ALU.add).then_inc(G["sumsq"], 1)
                dve.wait_ge(G["sumsq"], n + 1)
                dve.tensor_scalar(ss[:], ss[:], NORM_FLOOR, 0.5, ALU.max, ALU.mult).then_inc(G["clipped"], 1)
                dve.wait_ge(G["clipped"], n + 1)
                dve.tensor_scalar(rt[:].bitcast(I32), ss[:].bitcast(I32), 1, None,
                                  ALU.logical_shift_right).then_inc(G["halved"], 1)
                dve.wait_ge(G["halved"], n + 1)
                dve.tensor_scalar(rn[:].bitcast(I32), rt[:].bitcast(I32), -1.0, RSQRT_MAGIC_OF_HALF,
                                  ALU.mult, ALU.add).then_inc(G["seeded"], 1)

            def quad_max(s, q):
                if not is_sample(s):
                    return
                i = s * NQ + q
                dve.wait_ge(G["quad_scores"], i + 1)
                wait(dve, G["quad_probs"], i - 1)
                src = S[q % 2][:].rearrange("p (h c) -> p h c", h=QUAD)
                if causal:
                    dve.tensor_tensor(m.masked[q % 2][:], src, m.mask[:].unsqueeze(1).broadcast_to([P, QUAD, P]),
                                      ALU.add).then_inc(G["quad_masked"], 1)
                    dve.wait_ge(G["quad_masked"], i + 1)
                    src = m.masked[q % 2][:]
                dve.tensor_reduce(m.negmax[q % 2][:], src, AX.X, ALU.max, negate=True).then_inc(G["quad_negmax"], 1)

            def normalise(n, par):
                if not is_sample(n):
                    return
                dve.wait_ge(G["quad_out"], (n + 1) * NQ)
                wait(dve, G["o_ready"], n)
                dve.reciprocal(m.rec[:, 0:heads], m.rsum[par][:, 0:heads]).then_inc(G["rec_ready"], 1)
                dve.wait_ge(G["rec_ready"], n + 1)
                wait(dve, G["oT_bank"], n)
                dve.tensor_tensor(m.ob[:, 0:width].rearrange("p (h c) -> p h c", h=heads),
                                  heads_of(OB[:, 0:width]),
                                  m.rec[:, 0:heads].unsqueeze(2).broadcast_to([P, heads, dh]),
                                  ALU.mult).then_inc(G["o_ready"], 1)

            def statistics(n, pieces, kept, source):
                wait(dve, G["mv_kept"], n)
                for i, piece in enumerate(pieces):
                    dve.bn_stats(m.bn[:, i, :], piece).then_inc(G["stats"], 1)
                dve.wait_ge(G["stats"], len(pieces) * (n + 1))
                copy(kept, source).then_inc(G["kept"], 1)
                dve.bn_aggr(m.mv1[:], m.bn[:, 0:len(pieces), :].rearrange("p a b -> p (a b)")).then_inc(G["aggregated"], 1)
                dve.wait_ge(G["aggregated"], n + 1)
                copy(m.mv[:, n, :], m.mv1[:]).then_inc(G["mv_kept"], 1)

            def add_back(n, par):
                if not is_sample(n):
                    return
                dve.wait_ge(G["wo_bank"], n + 1)
                R = m.Y if local else m.X
                row = m.row[par]
                if local:
                    wait(dve, G["shifted"], n - 1)
                else:
                    wait(dve, G["mv_kept"], n)
                dve.tensor_tensor(row[:], WB[:, 0:D], R[:, n, :], ALU.add).then_inc(G["added"], 1)
                dve.wait_ge(G["added"], n + 1)
                if local:
                    copy(R[:, n, :], row[:]).then_inc(G["y_kept"], 1)
                    return
                if cross:
                    dve.tensor_tensor(row[:], row[:], m.b_cross[:, 3, :], ALU.add).then_inc(G["biased"], 1)
                    dve.wait_ge(G["biased"], n + 1)
                statistics(n, (row[:],), R[:, n, :], row[:])

            def shifted_stats(n, par):
                if not local or not is_sample(n):
                    return
                dve.wait_ge(G["shifted"], n + 1)
                statistics(n, (m.row[par][:, 0:P], TR1[:, 0:P]), m.YS[:, n, :], TR1[:, 0:P])

            if cross or (local and not layer):
                dve.tensor_scalar(m.vare[:], m.mv[:, :, 1], EPS, None, ALU.add).then_inc(G["start"], 1)
                dve.wait_ge(G["start"], 1)
                rsqrt(dve, m.rstd[:], m.vare[:], m.nt[:], G["start"], 1)
                dve.wait_ge(G["start"], 1 + RSQRT_OPS)
            if cross:
                dve.wait_ge(m.ld_cross, m.n_loads[m.ld_cross.name])
            if local:
                if not layer:
                    dve.wait_ge(m.ld_small, m.n_loads[m.ld_small.name])
                for w in range(2):
                    sc = m.qks[:, layer, w, :]
                    dve.tensor_tensor(m.rots[:, w, 0, :], m.rot[:, w, 0, :], sc, ALU.mult).then_inc(G["scaled"], 1)
                    for t in range(2):
                        lo, hi = t * dh // 2, (t + 1) * dh // 2
                        other = sc[:, (1 - t) * dh // 2:(2 - t) * dh // 2]
                        dve.tensor_tensor(m.rots[:, w, 1, lo:hi], m.rot[:, w, 1, lo:hi], other,
                                          ALU.mult).then_inc(G["scaled"], 1)
                dve.wait_ge(G["scaled"], 6)
            if local and not layer:
                for i in range(2):
                    dve.memset(m.kB[i][:], 0.0).then_inc(G["start"], 1)
                dve.memset(m.three_halves[:], 1.5).then_inc(G["start"], 1)
                dve.wait_ge(G["start"], 4 + RSQRT_OPS)
            if causal or cross:
                dve.wait_ge(m.ld_const, m.n_loads[m.ld_const.name])
            def read_kT(n, par, part):
                if not is_sample(n):
                    return
                dve.wait_ge(G["kT_bank"], n + 1)
                wait(dve, G["quad_scores"], (n - 1) * NQ)
                if local:
                    lo, hi = part * dh, (part + 1) * dh
                    dve.tensor_copy(key_blocks(par)[lo:hi, :, part * P:(part + 1) * P],
                                    TR1[lo:hi, :].rearrange("p (t c) -> p t c", t=4)).then_inc(G["kT_ready"], 1)
                else:
                    dve.tensor_tensor(m.kB[par][:, part, :].rearrange("p (h c) -> p h c", h=8),
                                      TR1[:, part * P:(part + 1) * P].unsqueeze(1).broadcast_to([P, 8, P]),
                                      m.own[:].unsqueeze(2).broadcast_to([P, 8, P]), ALU.mult).then_inc(G["kT_ready"], 1)

            def body(s, par):
                nxt = s + AHEAD
                for q in range(NQ):
                    if q == 0:
                        normed(nxt, par)
                    if q == 0 and local:
                        normalise(s - 2, par)
                    if q == 1 and local:
                        rotate(nxt, 0)
                        shifted_stats(s - 3, 1 - par)
                        rotate(nxt, 1)
                    if q == 2:
                        normalise(s - 1, 1 - par)
                    quad_max(s, q)
                    if q < 2 and not local:
                        read_kT(s + 1, 1 - par, q)
                    if local and q == 1:
                        norms(nxt, par)
                        for part in range(2):
                            read_kT(s + 1, 1 - par, part)
                        add_back(s - 2, par)
                    elif q == 2:
                        read_a(nxt, par)
                    elif q == 3:
                        read_b(nxt, par)
                        add_back(s - 1, 1 - par)

            over_samples(dve, body)

        @block.scalar
        def _(act):
            def read_xT(n, par):
                if not is_sample(n):
                    return
                act.wait_ge(G["xT_bank"], n + 1)
                wait(act, G["projC"] if local else G["projB"], n - 1)
                src = TR0[:, 0:nT * P].rearrange("p (t c) -> p t c", t=nT)
                if not local:
                    act.copy(m.xT[par][:, 0:nT, :], src).then_inc(G["xT_ready"], 1)
                    return
                act.copy(m.xT[par][:, 1, 1:P], src[:, 1, 0:P - 1]).then_inc(G["xT_ready"], 1)
                act.copy(m.xT[par][:, 0, :], src[:, 0, :]).then_inc(G["xT_ready"], 1)

            def read_qT(n, par):
                if not is_sample(n):
                    return
                act.wait_ge(G["qT_bank"], n + 1)
                wait(act, G["quad_scores"], (n - 1) * NQ)
                act.activation(m.qT[par][:, 0:OT_TILES, :],
                               TR0[:, 0:width].rearrange("p (t c) -> p t c", t=OT_TILES), ACT.Copy,
                               scale=1.0 if local else 0.25).then_inc(G["qT_ready"], 1)

            def square(n, which):
                if not is_sample(n):
                    return
                act.wait_ge(G["projB"] if which else G["projA"], n + 1)
                wait(act, G["rotated"], ROT * n)
                wait(act, G["sumsq"], n)
                done = G["evacB"] if which else G["evacA"]
                act.copy(m.raw[:, which, :], (PJ1 if which else PJ0)[:]).then_inc(done, 1)
                act.wait_ge(done, n + 1)
                act.activation(m.sq[:, which, :], m.raw[:, which, :], ACT.Square).then_inc(G["squared"], 1)

            def read_c(n):
                if not is_sample(n):
                    return
                act.wait_ge(G["projC"], n + 1)
                act.copy(m.V[:, n, :], PJ0[:]).then_inc(G["evacC"], 1)

            def read_pT(s, q):
                if not is_sample(s):
                    return
                i = s * NQ + q
                act.wait_ge(G["quad_pT_bank"], i + 1)
                wait(act, G["quad_out"], i - 1)
                act.copy(m.pT[q % 2][:], PTB[:].rearrange("p (h c) -> p h c", h=QUAD)).then_inc(G["quad_pT"], 1)

            def exponentials(s, par, q):
                if not is_sample(s):
                    return
                i = s * NQ + q
                act.wait_ge(G["quad_negmax"], i + 1)
                wait(act, G["quad_pT_bank"], i - 1)
                if q == 0:
                    wait(act, G["rec_ready"], s - 1)
                src = m.masked[q % 2] if causal else S[q % 2][:].rearrange("p (h c) -> p h c", h=QUAD)
                for j in range(QUAD):
                    h = QUAD * q + j
                    last = act.activation(m.probs[q % 2][:, j, :], src[:, j, :], ACT.Exp,
                                          bias=m.negmax[q % 2][:, j:j + 1],
                                          accum_out=m.rsum[par][:, h:h + 1])
                last.then_inc(G["quad_probs"], 1)

            def read_oT(n):
                if not is_sample(n):
                    return
                act.wait_ge(G["oT_bank"], n + 1)
                wait(act, G["wo_bank"], n)
                act.copy(m.oT[:, 0:OT_TILES, :],
                         TR1[:, 0:width].rearrange("p (t c) -> p t c", t=OT_TILES)).then_inc(G["oT_ready"], 1)

            if local:
                for i in range(2):
                    act.memzero(m.xT[i][:, 1, 0:1]).then_inc(G["zeroed"], 1)
                act.wait_ge(G["zeroed"], 2)
            def body(s, par):
                nxt = s + AHEAD
                for q in range(NQ):
                    if local and q == 0:
                        read_xT(nxt, par)
                    read_pT(*((s, q - LAG) if q >= LAG else (s - 1, NQ + q - LAG)))
                    if not local and q == 0:
                        read_qT(s + 1, 1 - par)
                        read_xT(nxt, par)
                    exponentials(s, par, q)
                    if local and q == 0:
                        read_oT(s - 2)
                        square(nxt, 0)
                        square(nxt, 1)
                    elif local:
                        read_c(nxt)
                        read_qT(s + 1, 1 - par)
                    elif q == 2:
                        read_oT(s - 1)

            over_samples(act, body)

        if local:
            @block.gpsimd
            def _(pool):
                def finish(n, par):
                    if not is_sample(n):
                        return
                    qk = m.qkb[par][:]
                    ss, y, t = m.ss[par][:], m.rn[par][:], m.rt[par][:]
                    wait(pool, G["kT_bank"], n - 1)
                    pool.wait_ge(G["rotated"], ROT * (n + 1))
                    pool.tensor_tensor(qk, m.ra, m.rb, ALU.add).then_inc(G["rotsum"], 1)
                    pool.wait_ge(G["seeded"], n + 1)
                    step = n * 4 * NEWTON
                    for i in range(NEWTON):
                        if i:
                            pool.wait_ge(G["newton"], step + 4 * i)
                        pool.tensor_tensor(t, y, y, ALU.mult).then_inc(G["newton"], 1)
                        pool.wait_ge(G["newton"], step + 4 * i + 1)
                        pool.tensor_tensor(t, t, ss, ALU.mult).then_inc(G["newton"], 1)
                        pool.wait_ge(G["newton"], step + 4 * i + 2)
                        pool.tensor_tensor(t, m.three_halves[:], t, ALU.subtract).then_inc(G["newton"], 1)
                        pool.wait_ge(G["newton"], step + 4 * i + 3)
                        pool.tensor_tensor(y, y, t, ALU.mult).then_inc(G["newton"], 1)
                    pool.wait_ge(G["newton"], step + 4 * NEWTON)
                    pool.wait_ge(G["rotsum"], n + 1)
                    split = qk.rearrange("p w (h c) -> p (w h) c", h=heads)
                    pool.tensor_tensor(split, split, y.unsqueeze(2).broadcast_to([P, 2 * heads, dh]),
                                       ALU.mult).then_inc(G["qk_ready"], 1)
                over_samples(pool, finish)

    release(nc, G)


def mlp(nc, m, layer, out):
    GS = m.GS
    NG = NS // GS
    N = GS * P
    final = layer == DEPTH - 1
    tag = f"mlp{layer}_"
    G = {n: nc.alloc_semaphore(name=tag + n) for n in (
        "start", "hn_ready", "hT_bank", "hT_ready", "tile_in", "gate_ready", "hid_ready", "out_bank",
        "biased", "added", "stored")}
    NORMS = 2 * GS
    A, GB, W2B, TB = m.banks[0:2], m.banks[2:4], m.banks[4:6], m.banks[6]

    def over_groups(eng, body):
        body(0)
        with eng.Fori(1, NG - 1, 1) as i:
            body(i)
        body(NG - 1)

    def is_group(i):
        return not isinstance(i, int) or i < NG

    with nc.Block() as block:
        @block.tensor
        def _(pe):
            def transposes(i):
                if not is_group(i):
                    return
                pe.wait_ge(G["hn_ready"], NORMS * (i + 1))
                wait(pe, G["hT_ready"], KT * i)
                for gs in range(GS):
                    for k in range(KT):
                        at = (gs * KT + k) * P
                        last = pe.transpose(TB[:, at:at + P], m.hn[:, gs, k * P:(k + 1) * P], m.ident[:])
                last.then_inc(G["hT_bank"], 1)

            pe.wait_ge(m.ld_mlp, m.n_loads[m.ld_mlp.name])
            transposes(0)

            def body(i):
                pe.wait_ge(G["hT_ready"], KT * (i + 1))
                for f, (lo, nf) in enumerate(TILES):
                    wait(pe, G["hid_ready"], i * FT + f - 1)
                    for bank, at in ((GB[f % 2], HID + lo), (A[f % 2], lo)):
                        for k in range(KT):
                            last = pe.matmul(bank[0:nf, 0:N], m.w_1[:, k, at:at + nf], m.hT[:, k, :],
                                             start=k == 0, stop=k == KT - 1)
                    last.then_inc(G["tile_in"], 1)
                transposes(i + 1)
                wait(pe, G["added"], GS * i)
                for f, (lo, nf) in enumerate(TILES):
                    pe.wait_ge(G["hid_ready"], i * FT + f + 1)
                    for gs in range(GS):
                        last = pe.matmul(W2B[gs][:, 0:D], m.hid[0:nf, f, gs * P:(gs + 1) * P],
                                         m.w_2[0:nf, f, :], start=f == 0, stop=f == FT - 1)
                last.then_inc(G["out_bank"], 1)

            over_groups(pe, body)

        @block.scalar
        def _(act):
            def body(i):
                for f, (lo, nf) in enumerate(TILES):
                    act.wait_ge(G["tile_in"], i * FT + f + 1)
                    wait(act, G["hid_ready"], i * FT + f - 1)
                    act.activation(m.gate[f % 2][0:nf, :], GB[f % 2][0:nf, 0:N], ACT.Gelu,
                                   bias=m.b_1[0:nf, layer, 1, f:f + 1]).then_inc(G["gate_ready"], 1)
            over_groups(act, body)

        @block.vector
        def _(dve):
            def normed(i):
                if not is_group(i):
                    return
                wait(dve, G["hT_bank"], i)
                for gs in range(GS):
                    for k, src in enumerate((m.Y, m.YS)):
                        s = i * GS + gs
                        dve.tensor_scalar(m.hn[:, gs, k * P:(k + 1) * P], src[:, s, 0:P], m.mv[:, s, 0:1],
                                          m.rstd[:, bass.ds(s, 1)], ALU.subtract, ALU.mult).then_inc(G["hn_ready"], 1)

            def read_hT(i):
                if not is_group(i):
                    return
                dve.wait_ge(G["hT_bank"], i + 1)
                wait(dve, G["tile_in"], FT * i)
                for k in range(KT):
                    dve.tensor_scalar(m.hT[:, k, :].rearrange("p (g c) -> p g c", g=GS),
                                      TB[:].rearrange("p (g k c) -> p k g c", g=GS, k=KT)[:, k],
                                      m.ln_g[:, layer, k:k + 1], m.ln_b[:, layer, k:k + 1],
                                      ALU.mult, ALU.add).then_inc(G["hT_ready"], 1)

            dve.tensor_scalar(m.vare[:], m.mv[:, :, 1], EPS, None, ALU.add).then_inc(G["start"], 1)
            dve.wait_ge(G["start"], 1)
            rsqrt(dve, m.rstd[:], m.vare[:], m.nt[:], G["start"], 1)
            dve.wait_ge(G["start"], 1 + RSQRT_OPS)
            normed(0)
            read_hT(0)
            normed(1)

            def body(i):
                for f, (lo, nf) in enumerate(TILES):
                    dve.wait_ge(G["gate_ready"], i * FT + f + 1)
                    wait(dve, G["out_bank"], i)
                    dve.scalar_tensor_tensor(m.hid[0:nf, f, :], A[f % 2][0:nf, 0:N], m.b_1[0:nf, layer, 0, f:f + 1],
                                             m.gate[f % 2][0:nf, :], ALU.add, ALU.mult).then_inc(G["hid_ready"], 1)
                read_hT(i + 1)
                normed(i + 2)
                dve.wait_ge(G["out_bank"], i + 1)
                dve.wait_ge(G["biased"], (1 + final) * (i + 1))
                for gs in range(GS):
                    s = i * GS + gs
                    dve.tensor_tensor(m.Y[:, s, :], W2B[gs][:, 0:D], m.Y[:, s, :], ALU.add).then_inc(G["added"], 1)

            body(0)
            with dve.Fori(1, NG - 2, 1) as i:
                body(i)
            body(NG - 2)
            body(NG - 1)

        @block.gpsimd
        def _(pool):
            def body(i):
                pool.wait_ge(G["hn_ready"], NORMS * (i + 1))
                y = m.Y[:, bass.ds(i * GS, GS), :]
                pool.tensor_tensor(y, y, m.b_2[:, layer, :].unsqueeze(1).broadcast_to([P, GS, D]),
                                   ALU.add).then_inc(G["biased"], 1)
                if final:
                    pool.wait_ge(G["biased"], 2 * i + 1)
                    pool.tensor_tensor(y, y, m.X[:, bass.ds(i * GS, GS), :], ALU.add).then_inc(G["biased"], 1)
            over_groups(pool, body)

        if final:
            @block.sync
            def _(sp):
                def body(i):
                    sp.wait_ge(G["added"], GS * (i + 1))
                    sp.dma_start(out.rearrange("s t d -> t s d")[:, bass.ds(i * GS, GS), :],
                                 m.Y[:, bass.ds(i * GS, GS), :]).then_inc(G["stored"], 16)
                over_groups(sp, body)
                sp.wait_ge(G["stored"], 16 * NG)
    release(nc, G)


def shape_constants():
    f = np.float32
    half = np.arange(0, DH, 2, dtype=f)
    inv_freq = (f(1.0) / f(10000.0) ** (half / f(DH))).astype(f)
    t = np.arange(P, dtype=f)
    freqs = t[:, None] * inv_freq[None, :]
    freqs = np.concatenate([freqs, freqs], -1)
    base = (half + f(0.4 * DH)) / f(1.4 * DH)
    power = (t - P // 2) / f(P // 2)
    scale = base[None, :] ** power[:, None]
    scale = np.concatenate([scale, scale], -1)
    sign = np.concatenate([-np.ones(DH // 2, f), np.ones(DH // 2, f)])[None, :]
    cos, sin = np.cos(freqs), np.sin(freqs) * sign
    rot = np.stack([np.stack([8.0 * cos * scale, 8.0 * sin * scale], 1),
                    np.stack([cos / scale, sin / scale], 1)], 1).astype(f)
    q, k = np.arange(P)[:, None], np.arange(P)[None, :]
    return {"c_ident": np.eye(P, dtype=f), "c_shift": (k == q + 1).astype(f),
            "c_mask": np.where(k <= q, 0.0, MASKED).astype(f), "c_rot": rot,
            "c_own": (q // 16 == np.arange(8)[None, :]).astype(f)}


def kernel(**inputs):
    import concourse.bacc as _bacc
    from concourse.bass_utils import run_bass_kernel_spmd as _run

    g = {k: np.asarray(v) for k, v in inputs.items()}

    def tiles(w):
        return w.reshape(-1, P, w.shape[-1]).transpose(1, 0, 2)

    arrays = {
        "x": g["x"], "ctx": g["ctx_1024"],
        "w_self": tiles(np.concatenate([g[f"L0_attn_W{c}"].reshape(D, D).T for c in "QKV"], 1)),
        "wo_self": tiles(g["L0_attn_WO"].transpose(0, 2, 1).reshape(D, D)),
        "w_cross": tiles(np.concatenate([g[f"L0_xattn_W_{c}"].T for c in "qkv"], 1)),
        "wo_cross": tiles(g["L0_xattn_W_o"].T),
        **{f"b_{c}": g[f"L0_xattn_b_{c}"].reshape(1, D) for c in "qkvo"},
        "w_qkv": np.stack([tiles(w) for w in g["L0_ffn_wqkv"]]),
        "wo_loc": np.stack([tiles(w) for w in g["L0_ffn_wo"]]),
        "w_1": np.stack([tiles(w) for w in g["L0_ffn_w1"]]),
        "w_2": g["L0_ffn_w2"],
        "b1": np.pad(g["L0_ffn_b1"].reshape(DEPTH, 2, HID), ((0, 0), (0, 0), (0, FT * P - HID)))
              .reshape(DEPTH, 2, FT, P).transpose(3, 0, 1, 2), "b2": g["L0_ffn_b2"],
        "ln_g": g["L0_ffn_ln_g"].reshape(DEPTH, KT, P).transpose(2, 0, 1),
        "ln_b": g["L0_ffn_ln_b"].reshape(DEPTH, KT, P).transpose(2, 0, 1),
        "q_scale": g["L0_ffn_q_scale"], "k_scale": g["L0_ffn_k_scale"],
        **shape_constants(),
    }
    arrays = {f"in_{k}": np.ascontiguousarray(v) for k, v in arrays.items()}
    nc = _bacc.Bacc("TRN2", target_bir_lowering=False, num_devices=1)
    args = {k[3:]: nc.dram_tensor(k, v.shape, mybir.dt.from_np(v.dtype), kind="ExternalInput").ap()
            for k, v in arrays.items()}
    out = nc.dram_tensor("out_0", (NS, P, D), F32, kind="ExternalOutput").ap()
    decoder_kernel(nc, args, out)
    r = _run(nc, [arrays], core_ids=[0])
    return r.results[0]["out_0"]
```

```python
from contextlib import ExitStack

import numpy as np

import concourse.bass as bass
from concourse import mybir

F32 = mybir.dt.float32
I32 = mybir.dt.int32
ALU = mybir.AluOpType
ACT = mybir.ActivationFunctionType
AX = mybir.AxisListType

P = 128
NS = 16
D = 256
KT = D // P
EPS = 1e-5
NORM_FLOOR = 1e-24
MASKED = -3.0e38
QUAD = 4
BANK = 512
DEPTH = 2
GS = 2
HEADS = 8
DH = 64
INNER = HEADS * DH
HID = int(D * 4 * 2 / 3)
FT = -(-HID // P)
TILES = [(i * P, min(P, HID - i * P)) for i in range(FT)]
RSQRT_MAGIC = float(0x5F3759DF)
RSQRT_MAGIC_OF_HALF = float(0x5F3759DF - 0x400000)
NEWTON = 3
RSQRT_OPS = 2 + 3 * NEWTON


def wait(eng, sem, count):
    if isinstance(count, int) and count <= 0:
        return
    eng.wait_ge(sem, count)


def fewest(a, b):
    return min(a, b) if isinstance(a, int) else a


def is_sample(n):
    return not isinstance(n, int) or 0 <= n < NS


AHEAD, BEHIND = 2, 3
LOOP_FROM = 4


def sample_is(n, k):
    return isinstance(n, int) and n == k


def run(eng, parts):
    def body(part, s, par):
        start, slot, n_slots = part
        for q in range(n_slots):
            slot(s, par, q)

    def both(part, following, s):
        n_slots, n_next = part[2], following[2]
        for q in range(n_slots):
            if n_next == n_slots:
                part[1](s, s % 2, q)
                following[1](s - NS, s % 2, q)
            else:
                part[1](s, s % 2, q)
                if q in (0, 2):
                    following[1](s - NS, s % 2, q // 2)

    def phase(part, following):
        for s in range(1, LOOP_FROM):
            body(part, s, s % 2)
        with eng.Fori(LOOP_FROM // 2, NS // 2 - 1) as pair:
            body(part, pair * 2, 0)
            body(part, pair * 2 + 1, 1)
        if following:
            following[0]()
            for s in range(NS - 2, NS + 1):
                both(part, following, s)
        else:
            for s in range(NS - 2, NS + BEHIND):
                body(part, s, s % 2)

    def groups(part, following):
        start, first, second = part
        n_groups = NS // GS
        start()
        first(0)
        second(0)
        if following:
            following[0]()
        with eng.Fori(1, n_groups - 2, 1) as i:
            first(i)
            second(i)
        for s, i in ((-2, n_groups - 2), (-1, n_groups - 1)):
            if following:
                following[1](s, s % 2, 0)
            first(i)
            if following:
                following[1](s, s % 2, 1)
            second(i)
        if following:
            body(following, 0, 0)

    if not isinstance(parts[0][2], int):
        groups(parts[0], parts[1] if len(parts) > 1 else None)
        if len(parts) > 1:
            phase(parts[1], None)
        return
    parts[0][0]()
    for s in range(-AHEAD, 1):
        body(parts[0], s, s % 2)
    for i, part in enumerate(parts):
        phase(part, parts[i + 1] if i + 1 < len(parts) else None)


def rsqrt(dve, y, x, t, sem, base):
    dve.tensor_scalar(t.bitcast(I32), x.bitcast(I32), 1, None, ALU.logical_shift_right).then_inc(sem, 1)
    dve.wait_ge(sem, base + 1)
    dve.tensor_scalar(y.bitcast(I32), t.bitcast(I32), -1.0, RSQRT_MAGIC, ALU.mult, ALU.add).then_inc(sem, 1)
    for i in range(NEWTON):
        dve.wait_ge(sem, base + 2 + 3 * i)
        dve.scalar_tensor_tensor(t, y, -0.5, y, ALU.mult, ALU.mult).then_inc(sem, 1)
        dve.wait_ge(sem, base + 3 + 3 * i)
        dve.tensor_tensor(t, t, x, ALU.mult).then_inc(sem, 1)
        dve.wait_ge(sem, base + 4 + 3 * i)
        dve.scalar_tensor_tensor(y, t, 1.5, y, ALU.add, ALU.mult).then_inc(sem, 1)


def decoder_kernel(nc, a, out):
    with ExitStack() as ctx:
        def sb(name, shape, dt=F32):
            return ctx.enter_context(nc.sbuf_tensor(name, shape, dt))

        def sem(name):
            return ctx.enter_context(nc.semaphore(name))

        X = sb("X", [P, NS, D])
        Y = sb("Y", [P, NS, D])
        YS = sb("YS", [P, NS, P])
        bn = sb("bn", [P, 2, 6])
        mv = sb("mv", [P, NS, 2])
        vare = sb("vare", [P, NS])
        rstd = sb("rstd", [P, NS])
        nt = sb("nt", [P, NS])

        w_self = sb("w_self", [P, KT, 3 * D])
        wo_self = sb("wo_self", [P, KT, D])
        w_cross = sb("w_cross", [P, KT, 3 * D])
        wo_cross = sb("wo_cross", [P, KT, D])
        b_cross = sb("b_cross", [P, 4, D])
        w_qkv = sb("w_qkv", [P, KT, 3 * INNER])
        wo_loc = sb("wo_loc", [P, INNER // P, D])
        w_1 = sb("w_1", [P, KT, 2 * HID])
        w_2 = sb("w_2", [P, FT, D])
        b_1 = sb("b_1", [P, DEPTH, 2, FT])
        b_2 = sb("b_2", [P, DEPTH, D])
        ln_g = sb("ln_g", [P, DEPTH, KT])
        ln_b = sb("ln_b", [P, DEPTH, KT])
        qks = sb("qks", [P, DEPTH, 2, DH])
        ident = sb("ident", [P, P])
        shift = sb("shift", [P, P])
        mask = sb("mask", [P, P])
        rot = sb("rot", [P, 2, 2, DH])
        rots = sb("rots", [P, 2, 2, DH])

        xn = [sb(f"xn{i}", [P, D]) for i in range(2)]
        cx = [sb(f"cx{i}", [P, D]) for i in range(2)]
        xT = [sb(f"xT{i}", [P, 2 * KT, P]) for i in range(2)]
        qkb = [sb(f"qkb{i}", [P, 2, INNER]) for i in range(2)]
        qT = [sb(f"qT{i}", [P, 4, P]) for i in range(2)]
        kB = [sb(f"kB{i}", [P, 2, 8 * P]) for i in range(2)]
        own = sb("own", [P, 8])
        V = sb("V", [P, NS, INNER])
        masked = [sb(f"masked{i}", [P, QUAD, P]) for i in range(2)]
        probs = [sb(f"probs{i}", [P, QUAD, P]) for i in range(2)]
        pT = [sb(f"pT{i}", [P, QUAD, P]) for i in range(2)]
        negmax = [sb(f"negmax{i}", [P, QUAD]) for i in range(2)]
        rsum = [sb(f"rsum{i}", [P, 16]) for i in range(2)]
        row = [sb(f"row{i}", [P, D]) for i in range(2)]
        mv1 = sb("mv1", [P, 2])
        rec = sb("rec", [P, 16])
        ob = sb("ob", [P, INNER])
        oT = sb("oT", [P, INNER // P, P])
        three_halves = sb("three_halves", [P, 16])
        raw = sb("raw", [P, 2, INNER])
        sq = sb("sq", [P, 2, INNER])
        rot_ab = sb("rot_ab", [P, 4, INNER])
        ra, rb = rot_ab[:, 0:2, :], rot_ab[:, 2:4, :]
        ss = [sb(f"ss{i}", [P, 16]) for i in range(2)]
        rn = [sb(f"rn{i}", [P, 16]) for i in range(2)]
        rt = [sb(f"rt{i}", [P, 16]) for i in range(2)]
        flat = [t[:].rearrange("p h c -> p (h c)") for t in (*masked, *probs, *pT)]
        hn = flat[0].rearrange("p (g d) -> p g d", g=GS)
        hT = flat[1].rearrange("p (k n) -> p k n", k=KT)
        gate, hid = ([t[:, i * GS * P:(i + 1) * GS * P] for t in tiles for i in range(2)]
                     for tiles in (flat[2:3], flat[3:6]))

        banks = [ctx.enter_context(nc.psum_tensor(f"bank{i}", [P, BANK], F32)) for i in range(8)]

        ld_x = [sem(f"ld_x{i}") for i in range(5)]
        ld_const = sem("ld_const")
        ld_self = sem("ld_self")
        ld_self_out = sem("ld_self_out")
        ld_ident = sem("ld_ident")
        ld_cross = sem("ld_cross")
        ld_loc = sem("ld_loc")
        ld_mlp = sem("ld_mlp")
        ld_small = sem("ld_small")
        n_loads = {}

        def load(eng, s, dst, src):
            eng.dma_start(dst, src).then_inc(s, 16)
            n_loads[s.name] = n_loads.get(s.name, 0) + 16

        def load_mlp(eng, s, l):
            full = HID // P * P
            load(eng, s, w_1[:], a["w_1"][l])
            load(eng, s, w_2[:, 0:HID // P, :], a["w_2"][l, 0:full, :].rearrange("(f p) d -> p f d", p=P))
            load(eng, s, w_2[0:HID - full, HID // P, :], a["w_2"][l, full:HID, :])

        x_t = a["x"].rearrange("s t d -> t s d")

        def first_loads(sp):
            sp.dma_start(X[:, 0:2, :], x_t[:, 0:2, :]).then_inc(ld_x[0], 16)
            load(sp, ld_ident, ident[:], a["c_ident"])
            load(sp, ld_self, w_self[:], a["w_self"])
            sp.dma_start(X[:, 2:4, :], x_t[:, 2:4, :]).then_inc(ld_x[4], 16)
            load(sp, ld_const, own[:], a["c_own"])
            load(sp, ld_const, mask[:], a["c_mask"])
            for i in range(1, 4):
                sp.dma_start(X[:, 4 * i:4 * i + 4, :], x_t[:, 4 * i:4 * i + 4, :]).then_inc(ld_x[i], 16)
            load(sp, ld_self_out, wo_self[:], a["wo_self"])
            load(sp, ld_cross, w_cross[:], a["w_cross"])
            load(sp, ld_cross, wo_cross[:], a["wo_cross"])
            for i, b in enumerate(("b_q", "b_k", "b_v", "b_o")):
                load(sp, ld_cross, b_cross[:, i, :], a[b].broadcast_to([P, D]))

        def later_loads(sp):
            load(sp, ld_loc, shift[:], a["c_shift"])
            load(sp, ld_loc, w_qkv[:], a["w_qkv"][0])
            load(sp, ld_loc, wo_loc[:], a["wo_loc"][0])
            load(sp, ld_small, rot[:], a["c_rot"])
            load(sp, ld_small, b_1[:], a["b1"])
            load(sp, ld_small, ln_g[:], a["ln_g"])
            load(sp, ld_small, ln_b[:], a["ln_b"])
            for l in range(DEPTH):
                load(sp, ld_small, qks[:, l, 0, :], a["q_scale"][l:l + 1, :].broadcast_to([P, DH]))
                load(sp, ld_small, qks[:, l, 1, :], a["k_scale"][l:l + 1, :].broadcast_to([P, DH]))
                load(sp, ld_small, b_2[:, l, :], a["b2"][l:l + 1, :].broadcast_to([P, D]))
            load_mlp(sp, ld_mlp, 0)

        m = Shared()
        m.three_halves, m.V, m.X, m.Y, m.YS = three_halves, V, X, Y, YS
        m.a, m.b_1, m.b_2, m.b_cross, m.banks, m.bn = a, b_1, b_2, b_cross, banks, bn
        m.cx, m.gate, m.hT, m.hid, m.hn, m.ident = cx, gate, hT, hid, hn, ident
        m.kB, m.ld_const, m.ld_cross, m.ld_loc, m.ld_mlp, m.ld_self = kB, ld_const, ld_cross, ld_loc, ld_mlp, ld_self
        m.ld_small, m.ln_b, m.ln_g, m.load_mlp, m.mask, m.masked = ld_small, ln_b, ln_g, load_mlp, mask, masked
        m.mv, m.mv1, m.n_loads, m.negmax, m.nt, m.oT = mv, mv1, n_loads, negmax, nt, oT
        m.ob, m.own, m.pT, m.probs, m.qT, m.qkb = ob, own, pT, probs, qT, qkb
        m.qks, m.ra, m.raw, m.rb, m.rec, m.rn = qks, ra, raw, rb, rec, rn
        m.rot, m.rots, m.row, m.rstd, m.rsum, m.rt = rot, rots, row, rstd, rsum, rt
        m.shift, m.sq, m.ss, m.vare, m.w_1, m.w_2 = shift, sq, ss, vare, w_1, w_2
        m.w_cross, m.w_qkv, m.w_self, m.wo_cross, m.wo_loc, m.wo_self = w_cross, w_qkv, w_self, wo_cross, wo_loc, wo_self
        m.xT, m.xn = xT, xn
        m.ld_self_out, m.ld_ident, m.ld_x = ld_self_out, ld_ident, ld_x
        m.first_loads, m.later_loads = first_loads, later_loads
        together(nc, [attention(nc, m, "self", 0), attention(nc, m, "cross", 0), attention(nc, m, "local", 0)])
        together(nc, [mlp(nc, m, 0, out), attention(nc, m, "local", 1)])
        together(nc, [mlp(nc, m, 1, out)])


class Shared:
    pass


class Phase:
    pass


def together(nc, phases):
    for before, behind in zip(phases, phases[1:]):
        before.next, behind.prev = behind, before
    with nc.Block() as block:
        @block.sync
        def _(sp):
            for ph in phases:
                ph.sync(sp)

        @block.tensor
        def _(pe):
            run(pe, [ph.tensor(pe) for ph in phases])

        @block.vector
        def _(dve):
            run(dve, [ph.vector(dve) for ph in phases])

        @block.scalar
        def _(act):
            run(act, [ph.scalar(act) for ph in phases])

        @block.gpsimd
        def _(pool):
            for ph in phases:
                ph.gpsimd(pool)

    for ph in phases:
        nc.clear_and_free_semaphores(list(ph.G.values()))
    nc.all_engine_barrier()


def attention(nc, m, kind, layer):
    a = m.a
    cross, local = kind == "cross", kind == "local"
    causal = not cross
    tag = f"{kind}{layer}_"
    heads, dh = (HEADS, DH) if local else (16, 16)
    per_tile = P // dh
    width = heads * dh
    NQ = heads // QUAD
    LAG = 2
    OUT = 2 if local else 1
    OT_TILES = width // P
    nT = 2 * KT if cross else KT

    PJ0, PJ1, TR0, TR1, S0, S1, PTB, OB = m.banks
    S = (S0, S1)
    WB = PJ1 if local else PJ0

    G = {n: nc.alloc_semaphore(name=tag + n) for n in (
        "xn_ready", "xT_bank", "xT_ready", "projA", "projB", "evacA", "evacB", "qT_bank", "kT_bank",
        "qT_ready", "kT_ready", "quad_scores", "quad_negmax", "quad_probs", "quad_pT_bank", "quad_pT",
        "quad_out", "rec_ready", "o_ready", "oT_bank", "oT_ready", "wo_bank", "added", "stats",
        "aggregated", "mv_kept", "kept", "start", "first", "constant",
        *(["quad_masked"] if causal else []),
        *(["qk_ready", "ctx0", "ctx1", "biased"] if cross else []),
        *(["qk_ready", "projC", "evacC", "squared", "rotated", "sumsq", "clipped", "halved", "seeded", "newton", "rotsum",
           "shifted", "y_kept", "scaled", "y_ready", "cleared", "zeroed", "weights"] if local else []))}
    ctx_in = (G["ctx0"], G["ctx1"]) if cross else None
    KR = 2
    XR = 2 if local else 1
    ROT = 6
    qk_done = G["qk_ready"] if cross or local else G["evacA"]

    def key_blocks(par):
        return m.kB[par][:].rearrange("p a b -> p (a b)").rearrange("p (t c) -> p t c", t=OT_TILES)

    ph = Phase()
    ph.G, ph.prev, ph.next, ph.KR, ph.XR, ph.frees = G, None, None, KR, XR, None
    ph.early_keys = 1 if local else 2
    QUADS_BEFORE = 16 // QUAD
    ALL_QUADS = NS * QUADS_BEFORE
    ph.lent = G["evacC"] if local else G["evacA"]

    def before(eng, name, count):
        if not ph.prev:
            return
        if ph.prev.frees is None:
            eng.wait_ge(ph.prev.G[name], count)
        else:
            for signal, total in ph.prev.frees.get(name, ()):
                eng.wait_ge(ph.prev.G[signal], total)

    def sync(sp):
        if kind == "self":
            m.first_loads(sp)
        if cross:
            for s in range(2):
                sp.dma_start(m.cx[s][:], a["ctx"][s]).then_inc(ctx_in[s], 16)
            m.later_loads(sp)
            with sp.Fori(1, NS // 2) as pair:
                for par in range(2):
                    s = pair * 2 + par
                    sp.wait_ge(G["xT_bank"], s - 1)
                    sp.dma_start(m.cx[par][:], a["ctx"][s]).then_inc(ctx_in[par], 16)
        if local and layer:
            sp.dma_start(m.w_qkv[:], a["w_qkv"][layer]).then_inc(G["weights"], 16)
            sp.dma_start(m.wo_loc[:], a["wo_loc"][layer]).then_inc(G["weights"], 16)
            before(sp, "w_mlp", 0)
            m.load_mlp(sp, m.ld_mlp, layer)

    def tensor(pe):
        w_in = m.w_qkv if local else m.w_cross if cross else m.w_self
        w_out = m.wo_loc if local else m.wo_cross if cross else m.wo_self

        def transpose_inputs(n, par):
            if not is_sample(n):
                return
            pe.wait_ge(G["xn_ready"], n + 1)
            if cross:
                pe.wait_ge(ctx_in[par], (n - par) * 8 + 16)
            if sample_is(n, 0):
                before(pe, "qT_ready", NS)
            wait(pe, G["xT_ready"], XR * n)
            wait(pe, G["qT_ready"], n - 1 if local else n)
            for i in range(nT):
                src = m.xn[par] if i < KT else m.cx[par]
                last = pe.transpose(TR0[:, i * P:(i + 1) * P], src[:, i % KT * P:(i % KT + 1) * P], m.ident[:])
            last.then_inc(G["xT_bank"], 1)

        def project(bank, par, lo, n_cols, signal, tiles=0):
            for k in range(KT):
                last = pe.matmul(bank[:, 0:n_cols], m.xT[par][:, tiles + k, :],
                                 w_in[:, k, lo:lo + n_cols], start=k == 0, stop=k == KT - 1)
            last.then_inc(signal, 1)

        def project_a(n, par):
            if not is_sample(n):
                return
            pe.wait_ge(G["xT_ready"], XR * (n + 1))
            if isinstance(n, int) and n <= 3:
                before(pe, "added", NS - 3 + n)
            if local:
                wait(pe, G["evacC"], n)
            else:
                wait(pe, G["evacA"], n)
                wait(pe, G["added"], n - 3)
            project(PJ0, par, 0, D if cross else 2 * D, G["projA"])

        def project_b(n, par):
            if not is_sample(n):
                return
            if sample_is(n, 0):
                before(pe, "evacB", NS)
            if not local:
                wait(pe, G["evacB"], n)
            else:
                wait(pe, G["evacB"], n)
                wait(pe, G["added"], n - 4)
                project(PJ1, par, INNER, INNER, G["projB"])
                return
            if cross:
                project(PJ1, par, D, 2 * D, G["projB"], KT)
            else:
                project(PJ1, par, 2 * D, D, G["projB"])

        def project_c(n, par):
            if not local or not is_sample(n):
                return
            pe.wait_ge(G["evacA"], n + 1)
            project(PJ0, par, 2 * INNER, INNER, G["projC"])

        def transpose_qk(n, par):
            if not is_sample(n):
                return
            pe.wait_ge(qk_done, n + 1)
            wait(pe, G["xT_ready"], XR * (fewest(n + 2, NS) if local else n + 1))
            for i in range(OT_TILES):
                last = pe.transpose(TR0[:, i * P:(i + 1) * P], m.qkb[par][:, 0, i * P:(i + 1) * P], m.ident[:])
            last.then_inc(G["qT_bank"], 1)
            wait(pe, G["kT_ready"], KR * n)
            wait(pe, G["oT_ready"], n - 2)
            if isinstance(n, int) and n <= 1 + cross:
                before(pe, "oT_ready", NS - 1 - cross + n)
            if local:
                wait(pe, G["kept"], n - 3)
            for i in range(OT_TILES):
                last = pe.transpose(TR1[:, i * P:(i + 1) * P], m.qkb[par][:, 1, i * P:(i + 1) * P], m.ident[:])
            last.then_inc(G["kT_bank"], 1)

        def scores(s, par, q):
            if not is_sample(s):
                return
            if q == 0:
                pe.wait_ge(G["qT_ready"], s + 1)
                pe.wait_ge(G["kT_ready"], KR * (s + 1))
                if sample_is(s, 0):
                    before(pe, "quad_probs", ALL_QUADS)
            wait(pe, G["quad_masked"] if causal else G["quad_probs"], s * NQ + q - 1)
            t, n_heads = (2 * q, 2) if local else (q // 2, QUAD)
            for i in range(QUAD // n_heads):
                at = 0 if local else q % 2 * QUAD * P
                last = pe.matmul(S[q % 2][:, i * n_heads * P:(i + 1) * n_heads * P], m.qT[par][:, t + i, :],
                                 key_blocks(par)[:, t + i, at:at + n_heads * P], start=True, stop=True)
            last.then_inc(G["quad_scores"], 1)

        def transpose_probs(s, q):
            if not is_sample(s):
                return
            pe.wait_ge(G["quad_probs"], s * NQ + q + 1)
            if sample_is(s * NQ + q, 0):
                before(pe, "quad_pT", ALL_QUADS)
            wait(pe, G["quad_pT"], s * NQ + q)
            for j in range(QUAD):
                last = pe.transpose(PTB[:, j * P:(j + 1) * P], m.probs[q % 2][:, j, :], m.ident[:])
            last.then_inc(G["quad_pT_bank"], 1)

        def attend(s, q):
            if not is_sample(s):
                return
            if q == 0:
                pe.wait_ge(G["evacC"] if local else G["evacB"], s + 1)
                wait(pe, G["o_ready"], s)
                if sample_is(s, 0):
                    before(pe, "o_ready", NS)
            pe.wait_ge(G["quad_pT"], s * NQ + q + 1)
            for j in range(QUAD):
                h = QUAD * q + j
                last = pe.matmul(OB[:, h * dh:(h + 1) * dh], m.pT[q % 2][:, j, :],
                                 m.V[:, s, h * dh:(h + 1) * dh], start=True, stop=True)
            last.then_inc(G["quad_out"], 1)

        def transpose_out(n):
            if not is_sample(n):
                return
            pe.wait_ge(G["o_ready"], n + 1)
            wait(pe, G["kT_ready"], KR * fewest(n + 3, NS))
            if local:
                wait(pe, G["kept"], n)
            wait(pe, G["oT_ready"], n)
            if ph.next and isinstance(n, int) and n > NS - 1 - ph.next.early_keys:
                pe.wait_ge(ph.next.G["kT_ready"], ph.next.KR * (n - (NS - 1) + ph.next.early_keys))
            for i in range(OT_TILES):
                last = pe.transpose(TR1[:, i * P:(i + 1) * P], m.ob[:, i * P:(i + 1) * P], m.ident[:])
            last.then_inc(G["oT_bank"], 1)

        def project_out(n):
            if not is_sample(n):
                return
            pe.wait_ge(G["oT_ready"], n + 1)
            wait(pe, G["evacB"] if local else G["evacA"], fewest(n + OUT + AHEAD + 1, NS))
            wait(pe, G["added"], n)
            if ph.next and isinstance(n, int) and n >= NS - 3:
                pe.wait_ge(ph.next.lent, n - (NS - 3) + 1)
            if kind == "self" and sample_is(n, 0):
                pe.wait_ge(m.ld_self_out, m.n_loads[m.ld_self_out.name])
            for i in range(OT_TILES):
                last = pe.matmul(WB[:, 0:D], m.oT[:, i, :], w_out[:, i, :],
                                 start=i == 0, stop=i == OT_TILES - 1)
            last.then_inc(G["wo_bank"], 1)

        def shift_tokens(n, par):
            if not local or not is_sample(n):
                return
            pe.wait_ge(G["added"], n + 1)
            wait(pe, G["kT_ready"], KR * fewest(n + 4, NS))
            pe.matmul(TR1[:, 0:P], m.shift[:], m.row[par][:, P:D], start=True, stop=True).then_inc(G["shifted"], 1)

        def start():
            pe.wait_ge(m.ld_ident, m.n_loads[m.ld_ident.name])
            if local and layer:
                pe.wait_ge(G["weights"], 32)
            else:
                ld = m.ld_loc if local else m.ld_cross if cross else m.ld_self
                pe.wait_ge(ld, m.n_loads[ld.name])

        def slot(s, par, q):
            nxt = s + AHEAD
            scores(s, par, q)
            before = (s, q - LAG) if q >= LAG else (s - 1, NQ + q - LAG)
            if local and q == 0:
                transpose_inputs(nxt, par)
                shift_tokens(s - 3, 1 - par)
            transpose_probs(*before)
            if local and q == 0:
                project_a(nxt, par)
                project_b(nxt, par)
                transpose_out(s - 2)
            elif local:
                project_c(nxt, par)
                transpose_qk(s + 1, 1 - par)
                project_out(s - 2)
            elif q == 0:
                transpose_qk(s + 1, 1 - par)
                transpose_inputs(nxt, par)
            elif q == 1:
                project_a(nxt, par)
            elif q == 2:
                project_b(nxt, par)
                transpose_out(s - 1)
            else:
                project_out(s - 1)
            attend(*before)

        return start, slot, NQ

    def vector(dve):
        def normed(n, par):
            if not is_sample(n):
                return
            wait(dve, G["xT_bank"], n - 1)
            if local and layer:
                copy(m.xn[par][:], m.Y[:, n, :]).then_inc(G["xn_ready"], 1)
                return
            dve.tensor_scalar(m.xn[par][:], m.X[:, n, :], m.mv[:, n, 0:1], m.rstd[:, bass.ds(n, 1)],
                              ALU.subtract, ALU.mult).then_inc(G["xn_ready"], 1)

        def keep_normed(n):
            if local and not layer and is_sample(n):
                dve.tensor_scalar(m.Y[:, n, :], m.X[:, n, :], m.mv[:, n, 0:1], m.rstd[:, bass.ds(n, 1)],
                                  ALU.subtract, ALU.mult).then_inc(G["y_ready"], 1)

        def copy(out, in_):
            return dve.tensor_scalar(out, in_, 1.0, None, ALU.mult)

        def heads_of(ap):
            return ap.rearrange("p (h c) -> p h c", h=heads)

        def read_a(n, par):
            if local or not is_sample(n):
                return
            dve.wait_ge(G["projA"], n + 1)
            if sample_is(n, 0):
                before(dve, "kT_bank", NS)
            wait(dve, G["kT_bank"], n - 1)
            if cross:
                dve.tensor_tensor(m.qkb[par][:, 0, 0:D], PJ0[:, 0:D], m.b_cross[:, 0, :], ALU.add).then_inc(G["evacA"], 1)
            else:
                dve.tensor_copy(m.qkb[par][:, :, 0:D], PJ0[:].rearrange("p (w c) -> p w c", w=2)).then_inc(G["evacA"], 1)

        def read_b(n, par):
            if not is_sample(n):
                return
            dve.wait_ge(G["projB"], n + 1)
            if cross:
                dve.tensor_tensor(m.qkb[par][:, 1, 0:D], PJ1[:, 0:D], m.b_cross[:, 1, :], ALU.add).then_inc(G["qk_ready"], 1)
                dve.tensor_tensor(m.V[:, n, 0:D], PJ1[:, D:2 * D], m.b_cross[:, 2, :], ALU.add).then_inc(G["evacB"], 1)
            else:
                copy(m.V[:, n, 0:D], PJ1[:, 0:D]).then_inc(G["evacB"], 1)

        def rotate(n, which):
            if not is_sample(n):
                return
            dve.wait_ge(G["evacB"] if which else G["evacA"], n + 1)
            wait(dve, G["rotsum"], n)

            def factor(kind, lo, hi):
                return m.rots[:, which, kind, lo:hi].unsqueeze(1).broadcast_to([P, heads, hi - lo])

            x, ra, rb = (heads_of(ap[:, which, :]) for ap in (m.raw, m.ra, m.rb))
            dve.tensor_tensor(ra, x, factor(0, 0, dh), ALU.mult).then_inc(G["rotated"], 1)
            for lo, hi in ((0, dh // 2), (dh // 2, dh)):
                dve.tensor_tensor(rb[:, :, lo:hi], x[:, :, dh // 2 - lo:dh - lo],
                                  factor(1, lo, hi), ALU.mult).then_inc(G["rotated"], 1)

        def norms(n, par):
            if not local or not is_sample(n):
                return [lambda: None] * 4
            ss, rn, rt = m.ss[par], m.rn[par], m.rt[par]

            def squares():
                wait(dve, G["qk_ready"], n - 1)
                dve.wait_ge(G["squared"], 2 * n + 2)
                dve.tensor_reduce(ss[:], m.sq[:].rearrange("p w (h c) -> p (w h) c", h=heads), AX.X,
                                  ALU.add).then_inc(G["sumsq"], 1)

            def clip():
                dve.wait_ge(G["sumsq"], n + 1)
                dve.tensor_scalar(ss[:], ss[:], NORM_FLOOR, 0.5, ALU.max, ALU.mult).then_inc(G["clipped"], 1)

            def halve():
                dve.wait_ge(G["clipped"], n + 1)
                dve.tensor_scalar(rt[:].bitcast(I32), ss[:].bitcast(I32), 1, None,
                                  ALU.logical_shift_right).then_inc(G["halved"], 1)

            def seed():
                dve.wait_ge(G["halved"], n + 1)
                dve.tensor_scalar(rn[:].bitcast(I32), rt[:].bitcast(I32), -1.0, RSQRT_MAGIC_OF_HALF,
                                  ALU.mult, ALU.add).then_inc(G["seeded"], 1)

            return squares, clip, halve, seed

        def quad_max(s, q):
            if not is_sample(s):
                return
            i = s * NQ + q
            dve.wait_ge(G["quad_scores"], i + 1)
            wait(dve, G["quad_probs"], i - 1)
            if sample_is(s * NQ + q, 0):
                before(dve, "quad_probs", ALL_QUADS)
                dve.wait_ge(m.ld_const, m.n_loads[m.ld_const.name])
            src = S[q % 2][:].rearrange("p (h c) -> p h c", h=QUAD)
            if causal:
                dve.tensor_tensor(m.masked[q % 2][:], src, m.mask[:].unsqueeze(1).broadcast_to([P, QUAD, P]),
                                  ALU.add).then_inc(G["quad_masked"], 1)
                dve.wait_ge(G["quad_masked"], i + 1)
                src = m.masked[q % 2][:]
            dve.tensor_reduce(m.negmax[q % 2][:], src, AX.X, ALU.max, negate=True).then_inc(G["quad_negmax"], 1)

        def normalise(n, par):
            if not is_sample(n):
                return
            dve.wait_ge(G["quad_out"], (n + 1) * NQ)
            wait(dve, G["o_ready"], n)
            if sample_is(n, 0):
                before(dve, "o_ready", NS)
                before(dve, "oT_bank", NS)
            dve.reciprocal(m.rec[:, 0:heads], m.rsum[par][:, 0:heads]).then_inc(G["rec_ready"], 1)
            dve.wait_ge(G["rec_ready"], n + 1)
            wait(dve, G["oT_bank"], n)
            dve.tensor_tensor(m.ob[:, 0:width].rearrange("p (h c) -> p h c", h=heads),
                              heads_of(OB[:, 0:width]),
                              m.rec[:, 0:heads].unsqueeze(2).broadcast_to([P, heads, dh]),
                              ALU.mult).then_inc(G["o_ready"], 1)

        def statistics(n, pieces, kept, source):
            wait(dve, G["mv_kept"], n)
            for i, piece in enumerate(pieces):
                dve.bn_stats(m.bn[:, i, :], piece).then_inc(G["stats"], 1)
            dve.wait_ge(G["stats"], len(pieces) * (n + 1))
            copy(kept, source).then_inc(G["kept"], 1)
            dve.bn_aggr(m.mv1[:], m.bn[:, 0:len(pieces), :].rearrange("p a b -> p (a b)")).then_inc(G["aggregated"], 1)
            dve.wait_ge(G["aggregated"], n + 1)
            copy(m.mv[:, n, :], m.mv1[:]).then_inc(G["mv_kept"], 1)

        def add_back(n, par):
            if not is_sample(n):
                return
            dve.wait_ge(G["wo_bank"], n + 1)
            if sample_is(n, 0):
                before(dve, "mv_kept", NS)
            R = m.Y if local else m.X
            row = m.row[par]
            if local:
                wait(dve, G["shifted"], n - 1)
            else:
                wait(dve, G["mv_kept"], n)
            dve.tensor_tensor(row[:], WB[:, 0:D], R[:, n, :], ALU.add).then_inc(G["added"], 1)
            dve.wait_ge(G["added"], n + 1)
            if local:
                copy(R[:, n, :], row[:]).then_inc(G["y_kept"], 1)
                return
            if cross:
                dve.tensor_tensor(row[:], row[:], m.b_cross[:, 3, :], ALU.add).then_inc(G["biased"], 1)
                dve.wait_ge(G["biased"], n + 1)
            statistics(n, (row[:],), R[:, n, :], row[:])

        def shifted_stats(n, par):
            if not local or not is_sample(n):
                return
            dve.wait_ge(G["shifted"], n + 1)
            statistics(n, (m.row[par][:, 0:P], TR1[:, 0:P]), m.YS[:, n, :], TR1[:, 0:P])

        def first_stats(lo, hi):
            for n in range(lo, hi):
                if n == 2 or n % 4 == 0:
                    dve.wait_ge(m.ld_x[4 if n == 2 else n // 4], 16)
                wait(dve, G["first"], 2 * n)
                dve.bn_stats(m.bn[:, 0, :], m.X[:, n, :]).then_inc(G["first"], 1)
                dve.wait_ge(G["first"], 2 * n + 1)
                dve.bn_aggr(m.mv[:, n, :], m.bn[:, 0, :]).then_inc(G["first"], 1)
            dve.wait_ge(G["first"], 2 * hi)

        def inverse_deviations(lo, hi):
            done = inverse_deviations.done
            wait(dve, G["start"], done)
            dve.tensor_scalar(m.vare[:, lo:hi], m.mv[:, lo:hi, 1], EPS, None, ALU.add).then_inc(G["start"], 1)
            dve.wait_ge(G["start"], done + 1)
            rsqrt(dve, m.rstd[:, lo:hi], m.vare[:, lo:hi], m.nt[:, lo:hi], G["start"], done + 1)
            inverse_deviations.done = done + 1 + RSQRT_OPS
            dve.wait_ge(G["start"], inverse_deviations.done)

        inverse_deviations.done = 0
        def start():
            if kind == "self":
                first_stats(0, 2)
                inverse_deviations(0, 2)
                return
            before(dve, "xT_bank", NS)
            if cross:
                dve.wait_ge(m.ld_cross, m.n_loads[m.ld_cross.name])
            if local:
                if not layer:
                    dve.wait_ge(m.ld_small, m.n_loads[m.ld_small.name])
                for w in range(2):
                    sc = m.qks[:, layer, w, :]
                    dve.tensor_tensor(m.rots[:, w, 0, :], m.rot[:, w, 0, :], sc, ALU.mult).then_inc(G["scaled"], 1)
                    for t in range(2):
                        lo, hi = t * dh // 2, (t + 1) * dh // 2
                        other = sc[:, (1 - t) * dh // 2:(2 - t) * dh // 2]
                        dve.tensor_tensor(m.rots[:, w, 1, lo:hi], m.rot[:, w, 1, lo:hi], other,
                                          ALU.mult).then_inc(G["scaled"], 1)
                dve.wait_ge(G["scaled"], 6)
            if ph.prev:
                for n in range(2):
                    normed(n, n)

        def more_statistics(s):
            if kind == "self":
                for k, (lo, hi) in enumerate(((2, 6), (6, 11), (11, NS))):
                    if sample_is(s, k - AHEAD):
                        first_stats(lo, hi)
                        inverse_deviations(lo, hi)
            elif ph.prev and not (local and layer):
                for first_body, (lo, hi) in ((-2, (2, NS - 3)), (2, (NS - 3, NS))):
                    if sample_is(s, first_body):
                        before(dve, "mv_kept", hi)
                        inverse_deviations(lo, hi)
            if ph.next and sample_is(s, 3):
                dve.wait_ge(G["mv_kept"], 2)
                inverse_deviations(0, 2)

        def read_kT(n, par, part):
            if not is_sample(n):
                return
            dve.wait_ge(G["kT_bank"], n + 1)
            wait(dve, G["quad_scores"], (n - 1) * NQ)
            if isinstance(n, int) and n <= 1:
                before(dve, "quad_scores", ALL_QUADS - QUADS_BEFORE * (1 - n))
            if local:
                if not layer and isinstance(n, int) and n <= 1:
                    dve.wait_ge(G["cleared"], 2 * n + 2)
                lo, hi = part * dh, (part + 1) * dh
                dve.tensor_copy(key_blocks(par)[lo:hi, :, part * P:(part + 1) * P],
                                TR1[lo:hi, :].rearrange("p (t c) -> p t c", t=4)).then_inc(G["kT_ready"], 1)
            else:
                dve.tensor_tensor(m.kB[par][:, part, :].rearrange("p (h c) -> p h c", h=8),
                                  TR1[:, part * P:(part + 1) * P].unsqueeze(1).broadcast_to([P, 8, P]),
                                  m.own[:].unsqueeze(2).broadcast_to([P, 8, P]), ALU.mult).then_inc(G["kT_ready"], 1)

        def slot(s, par, q):
            nxt = s + AHEAD
            if q == 0:
                if not (ph.prev and isinstance(nxt, int) and nxt <= 1):
                    normed(nxt, par)
                elif nxt >= 0:
                    keep_normed(nxt)
            if q == 1:
                more_statistics(s)
            if q == 0 and local:
                normalise(s - 2, par)
            if q == 1 and local:
                rotate(nxt, 0)
                rotate(nxt, 1)
                squares, clip, halve, seed = norms(nxt, par)
                squares()
            if q == 2:
                normalise(s - 1, 1 - par)
            quad_max(s, q)
            if q < 2 and not local:
                read_kT(s + 1, 1 - par, q)
            if local and q == 0:
                shifted_stats(s - 3, 1 - par)
                if not (isinstance(nxt, int) and nxt <= 1):
                    keep_normed(nxt)
            elif local:
                clip()
                halve()
                read_kT(s + 1, 1 - par, 0)
                seed()
                read_kT(s + 1, 1 - par, 1)
                add_back(s - 2, par)
            elif q == 2:
                read_a(nxt, par)
            elif q == 3:
                read_b(nxt, par)
                add_back(s - 1, 1 - par)

        return start, slot, NQ

    def scalar(act):
        def read_xT(n, par):
            if not is_sample(n):
                return
            act.wait_ge(G["xT_bank"], n + 1)
            if sample_is(n, 0):
                before(act, "projB", NS)
            wait(act, G["projC"] if local else G["projB"], n - 1)
            src = TR0[:, 0:nT * P].rearrange("p (t c) -> p t c", t=nT)
            if not local:
                act.copy(m.xT[par][:, 0:nT, :], src).then_inc(G["xT_ready"], 1)
                return
            act.copy(m.xT[par][:, 1, 1:P], src[:, 1, 0:P - 1]).then_inc(G["xT_ready"], 1)
            act.copy(m.xT[par][:, 0, :], src[:, 0, :]).then_inc(G["xT_ready"], 1)

        def read_qT(n, par):
            if not is_sample(n):
                return
            act.wait_ge(G["qT_bank"], n + 1)
            wait(act, G["quad_scores"], (n - 1) * NQ)
            if isinstance(n, int) and n <= 1:
                before(act, "quad_scores", ALL_QUADS - QUADS_BEFORE * (1 - n))
            act.activation(m.qT[par][:, 0:OT_TILES, :],
                           TR0[:, 0:width].rearrange("p (t c) -> p t c", t=OT_TILES), ACT.Copy,
                           scale=1.0 if local else 0.25).then_inc(G["qT_ready"], 1)

        def square(n, which):
            if not is_sample(n):
                return
            act.wait_ge(G["projB"] if which else G["projA"], n + 1)
            wait(act, G["rotated"], ROT * n)
            wait(act, G["sumsq"], n)
            done = G["evacB"] if which else G["evacA"]
            act.copy(m.raw[:, which, :], (PJ1 if which else PJ0)[:]).then_inc(done, 1)
            act.wait_ge(done, n + 1)
            act.activation(m.sq[:, which, :], m.raw[:, which, :], ACT.Square).then_inc(G["squared"], 1)

        def read_c(n):
            if not is_sample(n):
                return
            act.wait_ge(G["projC"], n + 1)
            act.copy(m.V[:, n, :], PJ0[:]).then_inc(G["evacC"], 1)

        def read_pT(s, q):
            if not is_sample(s):
                return
            i = s * NQ + q
            act.wait_ge(G["quad_pT_bank"], i + 1)
            wait(act, G["quad_out"], i - 1)
            if isinstance(i, int) and i <= 1:
                before(act, "quad_out", ALL_QUADS - 1 + i)
            act.copy(m.pT[q % 2][:], PTB[:].rearrange("p (h c) -> p h c", h=QUAD)).then_inc(G["quad_pT"], 1)

        def exponentials(s, par, q):
            if not is_sample(s):
                return
            i = s * NQ + q
            act.wait_ge(G["quad_negmax"], i + 1)
            wait(act, G["quad_pT_bank"], i - 1)
            if isinstance(i, int) and i <= 1:
                before(act, "quad_pT_bank", ALL_QUADS - 1 + i)
            if q == 0 and isinstance(s, int) and s <= 1:
                before(act, "rec_ready", NS - 1 + s)
            if q == 0:
                wait(act, G["rec_ready"], s - 1)
            src = m.masked[q % 2] if causal else S[q % 2][:].rearrange("p (h c) -> p h c", h=QUAD)
            for j in range(QUAD):
                h = QUAD * q + j
                last = act.activation(m.probs[q % 2][:, j, :], src[:, j, :], ACT.Exp,
                                      bias=m.negmax[q % 2][:, j:j + 1],
                                      accum_out=m.rsum[par][:, h:h + 1])
            last.then_inc(G["quad_probs"], 1)

        def read_oT(n):
            if not is_sample(n):
                return
            act.wait_ge(G["oT_bank"], n + 1)
            wait(act, G["wo_bank"], n)
            if sample_is(n, 0):
                before(act, "wo_bank", NS)
            act.copy(m.oT[:, 0:OT_TILES, :],
                     TR1[:, 0:width].rearrange("p (t c) -> p t c", t=OT_TILES)).then_inc(G["oT_ready"], 1)

        def start():
            if not local:
                return
            before(act, "projB", NS)
            for i in range(2):
                act.memzero(m.xT[i][:, 1, 0:1]).then_inc(G["zeroed"], 1)
            act.wait_ge(G["zeroed"], 2)

        def slot(s, par, q):
            nxt = s + AHEAD
            if local and q == 0:
                read_xT(nxt, par)
            read_pT(*((s, q - LAG) if q >= LAG else (s - 1, NQ + q - LAG)))
            if not local and q == 0:
                read_qT(s + 1, 1 - par)
                read_xT(nxt, par)
            if local and q == 0:
                square(nxt, 0)
            elif local:
                read_c(nxt)
                read_qT(s + 1, 1 - par)
            exponentials(s, par, q)
            if local and q == 0:
                square(nxt, 1)
                read_oT(s - 2)
            elif q == 2 and not local:
                read_oT(s - 1)

        return start, slot, NQ

    def gpsimd(pool):
        if kind == "self":
            pool.memset(m.three_halves[:], 1.5).then_inc(G["constant"], 1)
        if not local:
            return

        def finish(n, par):
            if not is_sample(n):
                return
            qk = m.qkb[par][:]
            ss, y, t = m.ss[par][:], m.rn[par][:], m.rt[par][:]
            wait(pool, G["kT_bank"], n - 1)
            if sample_is(n, 0):
                before(pool, "kT_bank", NS)
            pool.wait_ge(G["rotated"], ROT * (n + 1))
            pool.tensor_tensor(qk, m.ra, m.rb, ALU.add).then_inc(G["rotsum"], 1)
            pool.wait_ge(G["seeded"], n + 1)
            step = n * 4 * NEWTON
            for i in range(NEWTON):
                if i:
                    pool.wait_ge(G["newton"], step + 4 * i)
                pool.tensor_tensor(t, y, y, ALU.mult).then_inc(G["newton"], 1)
                pool.wait_ge(G["newton"], step + 4 * i + 1)
                pool.tensor_tensor(t, t, ss, ALU.mult).then_inc(G["newton"], 1)
                pool.wait_ge(G["newton"], step + 4 * i + 2)
                pool.tensor_tensor(t, m.three_halves[:], t, ALU.subtract).then_inc(G["newton"], 1)
                pool.wait_ge(G["newton"], step + 4 * i + 3)
                pool.tensor_tensor(y, y, t, ALU.mult).then_inc(G["newton"], 1)
            pool.wait_ge(G["newton"], step + 4 * NEWTON)
            pool.wait_ge(G["rotsum"], n + 1)
            split = qk.rearrange("p w (h c) -> p (w h) c", h=heads)
            pool.tensor_tensor(split, split, y.unsqueeze(2).broadcast_to([P, 2 * heads, dh]),
                               ALU.mult).then_inc(G["qk_ready"], 1)

        def clear():
            pool.wait_ge(G["qk_ready"], 1)
            for i in range(2):
                before(pool, "quad_scores", ALL_QUADS - QUADS_BEFORE * (1 - i))
                for part in range(2):
                    lo = (1 - part) * dh
                    wait(pool, G["cleared"], 2 * i + part)
                    pool.memset(key_blocks(i)[lo:lo + dh, :, part * P:(part + 1) * P], 0.0).then_inc(G["cleared"], 1)

        finish(0, 0)
        if not layer:
            clear()
            pool.wait_ge(G["cleared"], 4)
        finish(1, 1)
        with pool.Fori(1, NS // 2) as pair:
            finish(pair * 2, 0)
            finish(pair * 2 + 1, 1)

    ph.sync, ph.tensor, ph.vector, ph.scalar, ph.gpsimd = sync, tensor, vector, scalar, gpsimd
    return ph


def mlp(nc, m, layer, out):
    NG = NS // GS
    N = GS * P
    final = layer == DEPTH - 1
    tag = f"mlp{layer}_"
    G = {n: nc.alloc_semaphore(name=tag + n) for n in (
        "start", "hn_ready", "hT_bank", "hT_ready", "tile_in", "gate_ready", "hid_ready", "out_bank",
        "biased", "added", "stored")}
    NORMS = 2 * GS
    A, GB, W2B, TB = m.banks[0:2], m.banks[2:4], m.banks[4:6], m.banks[6]

    ph = Phase()
    ph.G, ph.prev, ph.next = G, None, None
    ph.frees = {"oT_ready": [("hid_ready", NG * FT)],
                "quad_probs": [("added", NS), ("tile_in", NG * FT), ("hT_bank", NG)],
                "quad_pT": [("hT_ready", KT * NG)], "quad_out": [("out_bank", NG)],
                "quad_pT_bank": [("hid_ready", NG * FT), ("out_bank", NG)],
                "xT_bank": [("added", GS)],
                "w_mlp": [("tile_in", NG * FT), ("out_bank", NG)]}

    def is_group(i):
        return not isinstance(i, int) or i < NG

    def tensor(pe):
        def transposes(i):
            if not is_group(i):
                return
            pe.wait_ge(G["hn_ready"], NORMS * (i + 1))
            wait(pe, G["hT_ready"], KT * i)
            for gs in range(GS):
                for k in range(KT):
                    at = (gs * KT + k) * P
                    last = pe.transpose(TB[:, at:at + P], m.hn[:, gs, k * P:(k + 1) * P], m.ident[:])
            last.then_inc(G["hT_bank"], 1)

        def start():
            pe.wait_ge(m.ld_mlp, 3 * 16 * (layer + 1))
            transposes(0)

        def first(i):
            behind = ph.next.G if ph.next and isinstance(i, int) and i >= NG - 2 else None
            pe.wait_ge(G["hT_ready"], KT * (i + 1))
            for f, (lo, nf) in enumerate(TILES):
                wait(pe, G["hid_ready"], i * FT + f - 1)
                if behind and f < 2:
                    n = i - (NG - 2) + 1
                    if f == 0:
                        pe.wait_ge(behind["xT_ready"], ph.next.XR * n)
                    pe.wait_ge(behind["evacB" if f else "evacA"], n)
                for bank, at in ((GB[f % 2], HID + lo), (A[f % 2], lo)):
                    for k in range(KT):
                        last = pe.matmul(bank[0:nf, 0:N], m.w_1[:, k, at:at + nf], m.hT[:, k, :],
                                         start=k == 0, stop=k == KT - 1)
                last.then_inc(G["tile_in"], 1)
            transposes(i + 1)
            if behind:
                pe.wait_ge(G["hid_ready"], i * FT + FT - 1)

        def second(i):
            wait(pe, G["added"], GS * i)
            for f, (lo, nf) in enumerate(TILES):
                pe.wait_ge(G["hid_ready"], i * FT + f + 1)
                for gs in range(GS):
                    last = pe.matmul(W2B[gs][:, 0:D], m.hid[f][0:nf, gs * P:(gs + 1) * P],
                                     m.w_2[0:nf, f, :], start=f == 0, stop=f == FT - 1)
            last.then_inc(G["out_bank"], 1)

        return start, first, second

    def scalar(act):
        def first(i):
            for f, (lo, nf) in enumerate(TILES):
                act.wait_ge(G["tile_in"], i * FT + f + 1)
                wait(act, G["hid_ready"], i * FT + f - 1)
                act.activation(m.gate[f % 2][0:nf, :], GB[f % 2][0:nf, 0:N], ACT.Gelu,
                               bias=m.b_1[0:nf, layer, 1, f:f + 1]).then_inc(G["gate_ready"], 1)

        return lambda: None, first, lambda i: None

    def vector(dve):
        def normed(i):
            if not is_group(i):
                return
            wait(dve, G["hT_bank"], i)
            for gs in range(GS):
                for k, src in enumerate((m.Y, m.YS)):
                    s = i * GS + gs
                    dve.tensor_scalar(m.hn[:, gs, k * P:(k + 1) * P], src[:, s, 0:P], m.mv[:, s, 0:1],
                                      m.rstd[:, bass.ds(s, 1)], ALU.subtract, ALU.mult).then_inc(G["hn_ready"], 1)

        def read_hT(i):
            if not is_group(i):
                return
            dve.wait_ge(G["hT_bank"], i + 1)
            wait(dve, G["tile_in"], FT * i)
            for k in range(KT):
                dve.tensor_scalar(m.hT[:, k, :].rearrange("p (g c) -> p g c", g=GS),
                                  TB[:].rearrange("p (g k c) -> p k g c", g=GS, k=KT)[:, k],
                                  m.ln_g[:, layer, k:k + 1], m.ln_b[:, layer, k:k + 1],
                                  ALU.mult, ALU.add).then_inc(G["hT_ready"], 1)

        def start():
            dve.tensor_scalar(m.vare[:], m.mv[:, :, 1], EPS, None, ALU.add).then_inc(G["start"], 1)
            dve.wait_ge(G["start"], 1)
            rsqrt(dve, m.rstd[:], m.vare[:], m.nt[:], G["start"], 1)
            dve.wait_ge(G["start"], 1 + RSQRT_OPS)
            normed(0)
            read_hT(0)
            normed(1)

        def first(i):
            for f, (lo, nf) in enumerate(TILES):
                dve.wait_ge(G["gate_ready"], i * FT + f + 1)
                wait(dve, G["out_bank"], i)
                dve.scalar_tensor_tensor(m.hid[f][0:nf, :], A[f % 2][0:nf, 0:N], m.b_1[0:nf, layer, 0, f:f + 1],
                                         m.gate[f % 2][0:nf, :], ALU.add, ALU.mult).then_inc(G["hid_ready"], 1)
            read_hT(i + 1)
            normed(i + 2)

        def second(i):
            dve.wait_ge(G["out_bank"], i + 1)
            dve.wait_ge(G["biased"], (1 + final) * (i + 1))
            for gs in range(GS):
                s = i * GS + gs
                dve.tensor_tensor(m.Y[:, s, :], W2B[gs][:, 0:D], m.Y[:, s, :], ALU.add).then_inc(G["added"], 1)

        return start, first, second

    def gpsimd(pool):
        def body(i):
            pool.wait_ge(G["hn_ready"], NORMS * (i + 1))
            y = m.Y[:, bass.ds(i * GS, GS), :]
            pool.tensor_tensor(y, y, m.b_2[:, layer, :].unsqueeze(1).broadcast_to([P, GS, D]),
                               ALU.add).then_inc(G["biased"], 1)
            if final:
                pool.wait_ge(G["biased"], 2 * i + 1)
                pool.tensor_tensor(y, y, m.X[:, bass.ds(i * GS, GS), :], ALU.add).then_inc(G["biased"], 1)

        with pool.Fori(0, NG, 1) as i:
            body(i)

    def sync(sp):
        if not final:
            return
        with sp.Fori(0, NG, 1) as i:
            sp.wait_ge(G["added"], GS * (i + 1))
            sp.dma_start(out.rearrange("s t d -> t s d")[:, bass.ds(i * GS, GS), :],
                         m.Y[:, bass.ds(i * GS, GS), :]).then_inc(G["stored"], 16)
        sp.wait_ge(G["stored"], 16 * NG)

    ph.sync, ph.tensor, ph.vector, ph.scalar, ph.gpsimd = sync, tensor, vector, scalar, gpsimd
    return ph


def shape_constants():
    f = np.float32
    half = np.arange(0, DH, 2, dtype=f)
    inv_freq = (f(1.0) / f(10000.0) ** (half / f(DH))).astype(f)
    t = np.arange(P, dtype=f)
    freqs = t[:, None] * inv_freq[None, :]
    freqs = np.concatenate([freqs, freqs], -1)
    base = (half + f(0.4 * DH)) / f(1.4 * DH)
    power = (t - P // 2) / f(P // 2)
    scale = base[None, :] ** power[:, None]
    scale = np.concatenate([scale, scale], -1)
    sign = np.concatenate([-np.ones(DH // 2, f), np.ones(DH // 2, f)])[None, :]
    cos, sin = np.cos(freqs), np.sin(freqs) * sign
    rot = np.stack([np.stack([8.0 * cos * scale, 8.0 * sin * scale], 1),
                    np.stack([cos / scale, sin / scale], 1)], 1).astype(f)
    q, k = np.arange(P)[:, None], np.arange(P)[None, :]
    return {"c_ident": np.eye(P, dtype=f), "c_shift": (k == q + 1).astype(f),
            "c_mask": np.where(k <= q, 0.0, MASKED).astype(f), "c_rot": rot,
            "c_own": (q // 16 == np.arange(8)[None, :]).astype(f)}


def kernel(**inputs):
    import concourse.bacc as _bacc
    from concourse.bass_utils import run_bass_kernel_spmd as _run

    g = {k: np.asarray(v) for k, v in inputs.items()}

    def tiles(w):
        return w.reshape(-1, P, w.shape[-1]).transpose(1, 0, 2)

    arrays = {
        "x": g["x"], "ctx": g["ctx_1024"],
        "w_self": tiles(np.concatenate([g[f"L0_attn_W{c}"].reshape(D, D).T for c in "QKV"], 1)),
        "wo_self": tiles(g["L0_attn_WO"].transpose(0, 2, 1).reshape(D, D)),
        "w_cross": tiles(np.concatenate([g[f"L0_xattn_W_{c}"].T for c in "qkv"], 1)),
        "wo_cross": tiles(g["L0_xattn_W_o"].T),
        **{f"b_{c}": g[f"L0_xattn_b_{c}"].reshape(1, D) for c in "qkvo"},
        "w_qkv": np.stack([tiles(w) for w in g["L0_ffn_wqkv"]]),
        "wo_loc": np.stack([tiles(w) for w in g["L0_ffn_wo"]]),
        "w_1": np.stack([tiles(w) for w in g["L0_ffn_w1"]]),
        "w_2": g["L0_ffn_w2"],
        "b1": np.pad(g["L0_ffn_b1"].reshape(DEPTH, 2, HID), ((0, 0), (0, 0), (0, FT * P - HID)))
              .reshape(DEPTH, 2, FT, P).transpose(3, 0, 1, 2), "b2": g["L0_ffn_b2"],
        "ln_g": g["L0_ffn_ln_g"].reshape(DEPTH, KT, P).transpose(2, 0, 1),
        "ln_b": g["L0_ffn_ln_b"].reshape(DEPTH, KT, P).transpose(2, 0, 1),
        "q_scale": g["L0_ffn_q_scale"], "k_scale": g["L0_ffn_k_scale"],
        **shape_constants(),
    }
    arrays = {f"in_{k}": np.ascontiguousarray(v) for k, v in arrays.items()}
    nc = _bacc.Bacc("TRN2", target_bir_lowering=False, num_devices=1)
    args = {k[3:]: nc.dram_tensor(k, v.shape, mybir.dt.from_np(v.dtype), kind="ExternalInput").ap()
            for k, v in arrays.items()}
    out = nc.dram_tensor("out_0", (NS, P, D), F32, kind="ExternalOutput").ap()
    decoder_kernel(nc, args, out)
    r = _run(nc, [arrays], core_ids=[0])
    return r.results[0]["out_0"]
```

```python
from contextlib import ExitStack

import numpy as np

import concourse.bass as bass
from concourse import mybir

F32 = mybir.dt.float32
I32 = mybir.dt.int32
ALU = mybir.AluOpType
ACT = mybir.ActivationFunctionType
AX = mybir.AxisListType

P = 128
NS = 16
D = 256
KT = D // P
EPS = 1e-5
NORM_FLOOR = 1e-24
MASKED = -3.0e38
QUAD = 4
BANK = 512
DEPTH = 2
GS = 2
HEADS = 8
DH = 64
INNER = HEADS * DH
HID = int(D * 4 * 2 / 3)
FT = -(-HID // P)
TILES = [(i * P, min(P, HID - i * P)) for i in range(FT)]
FULL = HID // P * P
REST = HID - FULL
GATES_AT = P // 2
MIXED = GATES_AT + REST
assert 0 < REST <= GATES_AT
RSQRT_MAGIC = float(0x5F3759DF)
RSQRT_MAGIC_OF_HALF = float(0x5F3759DF - 0x400000)
NEWTON = 3
RSQRT_OPS = 2 + 3 * NEWTON


def wait(eng, sem, count):
    if isinstance(count, int) and count <= 0:
        return
    eng.wait_ge(sem, count)


def fewest(a, b):
    return min(a, b) if isinstance(a, int) else a


def is_sample(n):
    return not isinstance(n, int) or 0 <= n < NS


AHEAD, BEHIND = 2, 3
LOOP_FROM = 4


def sample_is(n, k):
    return isinstance(n, int) and n == k


def run(eng, parts):
    def body(part, s, par):
        start, slot, n_slots, inputs = part
        for q in range(n_slots):
            slot(s, par, q)

    def both(part, following, s):
        n_slots, n_next = part[2], following[2]
        for q in range(n_slots):
            part[1](s, s % 2, q)
            if n_next == n_slots:
                following[1](s - NS, s % 2, q)
            elif q == 0:
                following[3](s - NS + AHEAD, s % 2)
            elif q < 3:
                following[1](s - NS, s % 2, q - 1, True)

    def attention_phase(part, following):
        for s in range(1, LOOP_FROM):
            body(part, s, s % 2)
        with eng.Fori(LOOP_FROM // 2, NS // 2 - 1) as pair:
            body(part, pair * 2, 0)
            body(part, pair * 2 + 1, 1)
        if following is None:
            for s in range(NS - 2, NS + BEHIND):
                body(part, s, s % 2)
        elif len(following) == 4:
            following[0]()
            for s in range(NS - 2, NS + 1):
                both(part, following, s)
        else:
            early, lead, between, ready = following[0:4]
            body(part, NS - 2, 0)
            body(part, NS - 1, 1)
            early()
            body(part, NS, 0)
            lead()
            part[1](NS + 1, 1, 0)
            between()
            part[1](NS + 1, 1, 1)
            body(part, NS + 2, 0)
            ready()

    def mlp_phase(part, following):
        first, second, late = part[4:]
        n_groups = NS // GS
        first(0)
        second(0)
        late()
        if following:
            following[0]()
        with eng.Fori(1, n_groups - 2, 1) as i:
            first(i)
            second(i)
        for s, i in ((-2, n_groups - 2), (-1, n_groups - 1)):
            if following:
                following[1](s, s % 2, 0)
            first(i)
            if following:
                following[1](s, s % 2, 1)
            second(i)
        if following:
            body(following, 0, 0)

    if len(parts[0]) == 4:
        parts[0][0]()
        for s in range(-AHEAD, 1):
            body(parts[0], s, s % 2)
    else:
        for piece in parts[0][0:4]:
            piece()
    for i, part in enumerate(parts):
        following = parts[i + 1] if i + 1 < len(parts) else None
        (attention_phase if len(part) == 4 else mlp_phase)(part, following)


def rsqrt(dve, y, x, t, sem, base):
    dve.tensor_scalar(t.bitcast(I32), x.bitcast(I32), 1, None, ALU.logical_shift_right).then_inc(sem, 1)
    dve.wait_ge(sem, base + 1)
    dve.tensor_scalar(y.bitcast(I32), t.bitcast(I32), -1.0, RSQRT_MAGIC, ALU.mult, ALU.add).then_inc(sem, 1)
    for i in range(NEWTON):
        dve.wait_ge(sem, base + 2 + 3 * i)
        dve.scalar_tensor_tensor(t, y, -0.5, y, ALU.mult, ALU.mult).then_inc(sem, 1)
        dve.wait_ge(sem, base + 3 + 3 * i)
        dve.tensor_tensor(t, t, x, ALU.mult).then_inc(sem, 1)
        dve.wait_ge(sem, base + 4 + 3 * i)
        dve.scalar_tensor_tensor(y, t, 1.5, y, ALU.add, ALU.mult).then_inc(sem, 1)


def decoder_kernel(nc, a, out):
    with ExitStack() as ctx:
        def sb(name, shape, dt=F32):
            return ctx.enter_context(nc.sbuf_tensor(name, shape, dt))

        def sem(name):
            return ctx.enter_context(nc.semaphore(name))

        X = sb("X", [P, NS, D])
        Y = sb("Y", [P, NS, D])
        YS = sb("YS", [P, NS, P])
        bn = sb("bn", [P, 2, 6])
        mv = sb("mv", [P, NS, 2])
        vare = sb("vare", [P, NS])
        rstd = sb("rstd", [P, NS])
        nt = sb("nt", [P, NS])

        w_self = sb("w_self", [P, KT, 3 * D])
        wo_self = sb("wo_self", [P, KT, D])
        w_cross = sb("w_cross", [P, KT, 3 * D])
        wo_cross = sb("wo_cross", [P, KT, D])
        b_cross = sb("b_cross", [P, 4, D])
        w_qkv = sb("w_qkv", [P, KT, 3 * INNER])
        wo_loc = sb("wo_loc", [P, INNER // P, D])
        w_1 = sb("w_1", [P, KT, 2 * FULL + MIXED])
        w_2 = sb("w_2", [P, FT, D])
        b_1 = sb("b_1", [P, DEPTH, 2, FT])
        b_2 = sb("b_2", [P, DEPTH, D])
        ln_g = sb("ln_g", [P, DEPTH, KT])
        ln_b = sb("ln_b", [P, DEPTH, KT])
        qks = sb("qks", [P, DEPTH, 2, DH])
        ident = sb("ident", [P, P])
        shift = sb("shift", [P, P])
        mask = sb("mask", [P, P])
        rot = sb("rot", [P, 2, 2, DH])
        rots = sb("rots", [P, 2, 2, DH])

        xn = [sb(f"xn{i}", [P, D]) for i in range(2)]
        cx = [sb(f"cx{i}", [P, D]) for i in range(2)]
        xT = [sb(f"xT{i}", [P, 2 * KT, P]) for i in range(2)]
        qkb = [sb(f"qkb{i}", [P, 2, INNER]) for i in range(2)]
        qT = [sb(f"qT{i}", [P, 4, P]) for i in range(2)]
        kB = [sb(f"kB{i}", [P, 2, 8 * P]) for i in range(2)]
        own = sb("own", [P, 8])
        V = sb("V", [P, NS, INNER])
        masked = [sb(f"masked{i}", [P, QUAD, P]) for i in range(2)]
        probs = [sb(f"probs{i}", [P, QUAD, P]) for i in range(2)]
        pT = [sb(f"pT{i}", [P, QUAD, P]) for i in range(2)]
        negmax = [sb(f"negmax{i}", [P, QUAD]) for i in range(2)]
        rsum = [sb(f"rsum{i}", [P, 16]) for i in range(2)]
        row = [sb(f"row{i}", [P, D]) for i in range(2)]
        mv1 = sb("mv1", [P, 2])
        rec = sb("rec", [P, 16])
        ob = sb("ob", [P, INNER])
        oT = sb("oT", [P, INNER // P, P])
        three_halves = sb("three_halves", [P, 16])
        raw = sb("raw", [P, 2, INNER])
        sq = sb("sq", [P, 2, INNER])
        rot_ab = sb("rot_ab", [P, 4, INNER])
        ra, rb = rot_ab[:, 0:2, :], rot_ab[:, 2:4, :]
        ss = [sb(f"ss{i}", [P, 16]) for i in range(2)]
        rn = [sb(f"rn{i}", [P, 16]) for i in range(2)]
        rt = [sb(f"rt{i}", [P, 16]) for i in range(2)]
        flat = [t[:].rearrange("p h c -> p (h c)") for t in (*masked, *probs, *pT)]
        hn = flat[0].rearrange("p (g d) -> p g d", g=GS)
        hT = flat[1].rearrange("p (k n) -> p k n", k=KT)
        gate, hid = ([t[:, i * GS * P:(i + 1) * GS * P] for t in tiles for i in range(2)]
                     for tiles in (flat[2:3], flat[3:6]))

        banks = [ctx.enter_context(nc.psum_tensor(f"bank{i}", [P, BANK], F32)) for i in range(8)]

        ld_x = [sem(f"ld_x{i}") for i in range(5)]
        ld_const = sem("ld_const")
        ld_self = sem("ld_self")
        ld_self_out = sem("ld_self_out")
        ld_ident = sem("ld_ident")
        ld_cross = sem("ld_cross")
        ld_loc = sem("ld_loc")
        ld_mlp = sem("ld_mlp")
        ld_small = sem("ld_small")
        n_loads = {}

        def load(eng, s, dst, src):
            eng.dma_start(dst, src).then_inc(s, 16)
            n_loads[s.name] = n_loads.get(s.name, 0) + 16

        def load_mlp(eng, s, l):
            load(eng, s, w_1[:], a["w_1"][l])
            load(eng, s, w_2[:, 0:HID // P, :], a["w_2"][l, 0:FULL, :].rearrange("(f p) d -> p f d", p=P))
            load(eng, s, w_2[0:REST, HID // P, :], a["w_2"][l, FULL:HID, :])

        x_t = a["x"].rearrange("s t d -> t s d")

        def first_loads(sp):
            sp.dma_start(X[:, 0:2, :], x_t[:, 0:2, :]).then_inc(ld_x[0], 16)
            load(sp, ld_ident, ident[:], a["c_ident"])
            load(sp, ld_self, w_self[:], a["w_self"])
            sp.dma_start(X[:, 2:4, :], x_t[:, 2:4, :]).then_inc(ld_x[4], 16)
            load(sp, ld_const, own[:], a["c_own"])
            load(sp, ld_const, mask[:], a["c_mask"])
            for i in range(1, 4):
                sp.dma_start(X[:, 4 * i:4 * i + 4, :], x_t[:, 4 * i:4 * i + 4, :]).then_inc(ld_x[i], 16)
            load(sp, ld_self_out, wo_self[:], a["wo_self"])
            load(sp, ld_cross, w_cross[:], a["w_cross"])
            load(sp, ld_cross, wo_cross[:], a["wo_cross"])
            for i, b in enumerate(("b_q", "b_k", "b_v", "b_o")):
                load(sp, ld_cross, b_cross[:, i, :], a[b].broadcast_to([P, D]))

        def later_loads(sp):
            load(sp, ld_loc, shift[:], a["c_shift"])
            load(sp, ld_loc, w_qkv[:], a["w_qkv"][0])
            load(sp, ld_loc, wo_loc[:], a["wo_loc"][0])
            load(sp, ld_small, rot[:], a["c_rot"])
            load(sp, ld_small, b_1[:], a["b1"])
            load(sp, ld_small, ln_g[:], a["ln_g"])
            load(sp, ld_small, ln_b[:], a["ln_b"])
            for l in range(DEPTH):
                load(sp, ld_small, qks[:, l, 0, :], a["q_scale"][l:l + 1, :].broadcast_to([P, DH]))
                load(sp, ld_small, qks[:, l, 1, :], a["k_scale"][l:l + 1, :].broadcast_to([P, DH]))
                load(sp, ld_small, b_2[:, l, :], a["b2"][l:l + 1, :].broadcast_to([P, D]))
            load_mlp(sp, ld_mlp, 0)

        m = Shared()
        m.three_halves, m.V, m.X, m.Y, m.YS = three_halves, V, X, Y, YS
        m.a, m.b_1, m.b_2, m.b_cross, m.banks, m.bn = a, b_1, b_2, b_cross, banks, bn
        m.cx, m.gate, m.hT, m.hid, m.hn, m.ident = cx, gate, hT, hid, hn, ident
        m.kB, m.ld_const, m.ld_cross, m.ld_loc, m.ld_mlp, m.ld_self = kB, ld_const, ld_cross, ld_loc, ld_mlp, ld_self
        m.ld_small, m.ln_b, m.ln_g, m.load_mlp, m.mask, m.masked = ld_small, ln_b, ln_g, load_mlp, mask, masked
        m.mv, m.mv1, m.n_loads, m.negmax, m.nt, m.oT = mv, mv1, n_loads, negmax, nt, oT
        m.ob, m.own, m.pT, m.probs, m.qT, m.qkb = ob, own, pT, probs, qT, qkb
        m.qks, m.ra, m.raw, m.rb, m.rec, m.rn = qks, ra, raw, rb, rec, rn
        m.rot, m.rots, m.row, m.rstd, m.rsum, m.rt = rot, rots, row, rstd, rsum, rt
        m.shift, m.sq, m.ss, m.vare, m.w_1, m.w_2 = shift, sq, ss, vare, w_1, w_2
        m.w_cross, m.w_qkv, m.w_self, m.wo_cross, m.wo_loc, m.wo_self = w_cross, w_qkv, w_self, wo_cross, wo_loc, wo_self
        m.xT, m.xn = xT, xn
        m.ld_self_out, m.ld_ident, m.ld_x = ld_self_out, ld_ident, ld_x
        m.first_loads, m.later_loads = first_loads, later_loads
        together(nc, [attention(nc, m, "self", 0), attention(nc, m, "cross", 0),
                      attention(nc, m, "local", 0)])
        together(nc, [mlp(nc, m, 0, out), attention(nc, m, "local", 1), mlp(nc, m, 1, out)])


def nothing(*unused):
    pass


class Shared:
    pass


class Phase:
    pass


def together(nc, phases):
    for before, behind in zip(phases, phases[1:]):
        before.next, behind.prev = behind, before
    with nc.Block() as block:
        @block.sync
        def _(sp):
            for ph in phases:
                ph.sync(sp)

        @block.tensor
        def _(pe):
            run(pe, [ph.tensor(pe) for ph in phases])

        @block.vector
        def _(dve):
            run(dve, [ph.vector(dve) for ph in phases])

        @block.scalar
        def _(act):
            run(act, [ph.scalar(act) for ph in phases])

        @block.gpsimd
        def _(pool):
            for ph in phases:
                ph.gpsimd(pool)

    for ph in phases:
        nc.clear_and_free_semaphores(list(ph.G.values()))
    nc.all_engine_barrier()


def attention(nc, m, kind, layer):
    a = m.a
    cross, local = kind == "cross", kind == "local"
    causal = not cross
    tag = f"{kind}{layer}_"
    heads, dh = (HEADS, DH) if local else (16, 16)
    width = heads * dh
    NQ = heads // QUAD
    LAG = 2
    OUT = 2 if local else 1
    OT_TILES = width // P
    nT = 2 * KT if cross else KT

    PJ0, PJ1, TR0, TR1, S0, S1, PTB, OB = m.banks
    S = (S0, S1)
    WB = PJ1 if local else PJ0

    G = {n: nc.alloc_semaphore(name=tag + n) for n in (
        "xn_ready", "xT_bank", "xT_ready", "projA", "projB", "evacA", "evacB", "qT_bank", "kT_bank",
        "qT_ready", "kT_ready", "quad_scores", "quad_negmax", "quad_probs", "quad_pT_bank", "quad_pT",
        "quad_out", "rec_ready", "o_ready", "oT_bank", "oT_ready", "wo_bank", "added", "stats",
        "aggregated", "mv_kept", "kept", "start", "first",
        *(["quad_masked"] if causal else []),
        *(["qk_ready", "ctx0", "ctx1", "biased"] if cross else []),
        *(["qk_ready", "projC", "evacC", "squared", "rotated", "sumsq", "clipped", "halved", "seeded", "newton", "rotsum",
           "shifted", "y_kept", "scaled", "y_ready", "constant", "cleared", "zeroed", "weights"] if local else []))}
    ctx_in = (G["ctx0"], G["ctx1"]) if cross else None
    KR = 2
    XR = 2 if local else 1
    ROT = 6
    qk_done = G["qk_ready"] if cross or local else G["evacA"]

    def key_blocks(par):
        return m.kB[par][:].rearrange("p a b -> p (a b)").rearrange("p (t c) -> p t c", t=OT_TILES)

    ph = Phase()
    ph.G, ph.prev, ph.next, ph.KR, ph.XR, ph.frees = G, None, None, KR, XR, None
    ph.early_keys = 1 if local else 2
    QUADS_BEFORE = 16 // QUAD
    ALL_QUADS = NS * QUADS_BEFORE
    ph.lent = G["evacC"] if local else G["evacA"]

    def before(eng, name, count):
        if not ph.prev:
            return
        if ph.prev.frees is None:
            eng.wait_ge(ph.prev.G[name], count)
        else:
            for signal, total in ph.prev.frees.get(name, ()):
                eng.wait_ge(ph.prev.G[signal], total)

    def sync(sp):
        if kind == "self":
            m.first_loads(sp)
        if cross:
            for s in range(2):
                sp.dma_start(m.cx[s][:], a["ctx"][s]).then_inc(ctx_in[s], 16)
            m.later_loads(sp)
            with sp.Fori(1, NS // 2) as pair:
                for par in range(2):
                    s = pair * 2 + par
                    sp.wait_ge(G["xT_bank"], s - 1)
                    sp.dma_start(m.cx[par][:], a["ctx"][s]).then_inc(ctx_in[par], 16)
        if local and layer:
            sp.dma_start(m.w_qkv[:], a["w_qkv"][layer]).then_inc(G["weights"], 16)
            sp.dma_start(m.wo_loc[:], a["wo_loc"][layer]).then_inc(G["weights"], 16)
            before(sp, "w_mlp", 0)
            m.load_mlp(sp, m.ld_mlp, layer)

    def tensor(pe):
        heir = ph.next if ph.next and ph.next.frees is None else None
        w_in = m.w_qkv if local else m.w_cross if cross else m.w_self
        w_out = m.wo_loc if local else m.wo_cross if cross else m.wo_self

        def transpose_inputs(n, par):
            if not is_sample(n):
                return
            pe.wait_ge(G["xn_ready"], n + 1)
            if cross:
                pe.wait_ge(ctx_in[par], (n - par) * 8 + 16)
            if sample_is(n, 0):
                before(pe, "qT_ready", NS)
            wait(pe, G["xT_ready"], XR * n)
            wait(pe, G["qT_ready"], n - 1 if local else n)
            for i in range(nT):
                src = m.xn[par] if i < KT else m.cx[par]
                last = pe.transpose(TR0[:, i * P:(i + 1) * P], src[:, i % KT * P:(i % KT + 1) * P], m.ident[:])
            last.then_inc(G["xT_bank"], 1)

        def project(bank, par, lo, n_cols, signal, tiles=0):
            for k in range(KT):
                last = pe.matmul(bank[:, 0:n_cols], m.xT[par][:, tiles + k, :],
                                 w_in[:, k, lo:lo + n_cols], start=k == 0, stop=k == KT - 1)
            last.then_inc(signal, 1)

        def project_a(n, par):
            if not is_sample(n):
                return
            pe.wait_ge(G["xT_ready"], XR * (n + 1))
            if isinstance(n, int) and n <= 3:
                before(pe, "added", NS - 3 + n)
            if local:
                wait(pe, G["evacC"], n)
            else:
                wait(pe, G["evacA"], n)
                wait(pe, G["added"], n - 3)
            project(PJ0, par, 0, D if cross else 2 * D, G["projA"])

        def project_b(n, par):
            if not is_sample(n):
                return
            if sample_is(n, 0):
                before(pe, "evacB", NS)
            if not local:
                wait(pe, G["evacB"], n)
            else:
                wait(pe, G["evacB"], n)
                wait(pe, G["added"], n - 4)
                project(PJ1, par, INNER, INNER, G["projB"])
                return
            if cross:
                project(PJ1, par, D, 2 * D, G["projB"], KT)
            else:
                project(PJ1, par, 2 * D, D, G["projB"])

        def project_c(n, par):
            if not local or not is_sample(n):
                return
            pe.wait_ge(G["evacA"], n + 1)
            project(PJ0, par, 2 * INNER, INNER, G["projC"])

        def transpose_qk(n, par):
            if not is_sample(n):
                return
            pe.wait_ge(qk_done, n + 1)
            wait(pe, G["xT_ready"], XR * (fewest(n + 2, NS) if local else n + 1))
            for i in range(OT_TILES):
                last = pe.transpose(TR0[:, i * P:(i + 1) * P], m.qkb[par][:, 0, i * P:(i + 1) * P], m.ident[:])
            last.then_inc(G["qT_bank"], 1)
            wait(pe, G["kT_ready"], KR * n)
            wait(pe, G["oT_ready"], n - 2)
            if isinstance(n, int) and n <= 1 + cross:
                before(pe, "oT_ready", NS - 1 - cross + n)
            if local:
                wait(pe, G["kept"], n - 3)
            for i in range(OT_TILES):
                last = pe.transpose(TR1[:, i * P:(i + 1) * P], m.qkb[par][:, 1, i * P:(i + 1) * P], m.ident[:])
            last.then_inc(G["kT_bank"], 1)

        def scores(s, par, q):
            if not is_sample(s):
                return
            if q == 0:
                pe.wait_ge(G["qT_ready"], s + 1)
                pe.wait_ge(G["kT_ready"], KR * (s + 1))
                if sample_is(s, 0):
                    before(pe, "quad_probs", ALL_QUADS)
            wait(pe, G["quad_masked"] if causal else G["quad_probs"], s * NQ + q - 1)
            t, n_heads = (2 * q, 2) if local else (q // 2, QUAD)
            for i in range(QUAD // n_heads):
                at = 0 if local else q % 2 * QUAD * P
                last = pe.matmul(S[q % 2][:, i * n_heads * P:(i + 1) * n_heads * P], m.qT[par][:, t + i, :],
                                 key_blocks(par)[:, t + i, at:at + n_heads * P], start=True, stop=True)
            last.then_inc(G["quad_scores"], 1)

        def transpose_probs(s, q):
            if not is_sample(s):
                return
            pe.wait_ge(G["quad_probs"], s * NQ + q + 1)
            if sample_is(s * NQ + q, 0):
                before(pe, "quad_pT", ALL_QUADS)
            wait(pe, G["quad_pT"], s * NQ + q)
            for j in range(QUAD):
                last = pe.transpose(PTB[:, j * P:(j + 1) * P], m.probs[q % 2][:, j, :], m.ident[:])
            last.then_inc(G["quad_pT_bank"], 1)

        def attend(s, q):
            if not is_sample(s):
                return
            if q == 0:
                pe.wait_ge(G["evacC"] if local else G["evacB"], s + 1)
                wait(pe, G["o_ready"], s)
                if sample_is(s, 0):
                    before(pe, "o_ready", NS)
            pe.wait_ge(G["quad_pT"], s * NQ + q + 1)
            for j in range(QUAD):
                h = QUAD * q + j
                last = pe.matmul(OB[:, h * dh:(h + 1) * dh], m.pT[q % 2][:, j, :],
                                 m.V[:, s, h * dh:(h + 1) * dh], start=True, stop=True)
            last.then_inc(G["quad_out"], 1)

        def transpose_out(n):
            if not is_sample(n):
                return
            pe.wait_ge(G["o_ready"], n + 1)
            wait(pe, G["kT_ready"], KR * fewest(n + 3, NS))
            if local:
                wait(pe, G["kept"], n)
            wait(pe, G["oT_ready"], n)
            if heir and isinstance(n, int) and n > NS - 1 - heir.early_keys:
                pe.wait_ge(heir.G["kT_ready"], heir.KR * (n - (NS - 1) + heir.early_keys))
            for i in range(OT_TILES):
                last = pe.transpose(TR1[:, i * P:(i + 1) * P], m.ob[:, i * P:(i + 1) * P], m.ident[:])
            last.then_inc(G["oT_bank"], 1)

        def project_out(n):
            if not is_sample(n):
                return
            pe.wait_ge(G["oT_ready"], n + 1)
            wait(pe, G["evacB"] if local else G["evacA"], fewest(n + OUT + AHEAD + 1, NS))
            wait(pe, G["added"], n)
            if heir and isinstance(n, int) and n >= NS - 3:
                pe.wait_ge(heir.lent, n - (NS - 3) + 1)
            if kind == "self" and sample_is(n, 0):
                pe.wait_ge(m.ld_self_out, m.n_loads[m.ld_self_out.name])
            for i in range(OT_TILES):
                last = pe.matmul(WB[:, 0:D], m.oT[:, i, :], w_out[:, i, :],
                                 start=i == 0, stop=i == OT_TILES - 1)
            last.then_inc(G["wo_bank"], 1)

        def shift_tokens(n, par):
            if not local or not is_sample(n):
                return
            pe.wait_ge(G["added"], n + 1)
            wait(pe, G["kT_ready"], KR * fewest(n + 4, NS))
            pe.matmul(TR1[:, 0:P], m.shift[:], m.row[par][:, P:D], start=True, stop=True).then_inc(G["shifted"], 1)

        def start():
            pe.wait_ge(m.ld_ident, m.n_loads[m.ld_ident.name])
            if local and layer:
                pe.wait_ge(G["weights"], 32)
            else:
                ld = m.ld_loc if local else m.ld_cross if cross else m.ld_self
                pe.wait_ge(ld, m.n_loads[ld.name])

        def slot(s, par, q, inputs_done=False):
            nxt = s + AHEAD
            scores(s, par, q)
            before = (s, q - LAG) if q >= LAG else (s - 1, NQ + q - LAG)
            if local and q == 0:
                if not inputs_done:
                    transpose_inputs(nxt, par)
                shift_tokens(s - 3, 1 - par)
            transpose_probs(*before)
            if local and q == 0:
                project_a(nxt, par)
                project_b(nxt, par)
                transpose_out(s - 2)
            elif local:
                project_c(nxt, par)
                transpose_qk(s + 1, 1 - par)
                project_out(s - 2)
            elif q == 0:
                transpose_qk(s + 1, 1 - par)
                if cross:
                    transpose_inputs(nxt, par)
            elif q == 1:
                project_a(nxt, par)
            elif q == 2:
                project_b(nxt, par)
                transpose_out(s - 1)
            else:
                project_out(s - 1)
            attend(*before)
            if q == 0 and kind == "self":
                transpose_inputs(nxt, par)

        return start, slot, NQ, transpose_inputs

    def vector(dve):
        def normed(n, par):
            if not is_sample(n):
                return
            wait(dve, G["xT_bank"], n - 1)
            if local and layer:
                copy(m.xn[par][:], m.Y[:, n, :]).then_inc(G["xn_ready"], 1)
                return
            dve.tensor_scalar(m.xn[par][:], m.X[:, n, :], m.mv[:, n, 0:1], m.rstd[:, bass.ds(n, 1)],
                              ALU.subtract, ALU.mult).then_inc(G["xn_ready"], 1)

        def keep_normed(n):
            if local and not layer and is_sample(n):
                dve.tensor_scalar(m.Y[:, n, :], m.X[:, n, :], m.mv[:, n, 0:1], m.rstd[:, bass.ds(n, 1)],
                                  ALU.subtract, ALU.mult).then_inc(G["y_ready"], 1)

        def copy(out, in_):
            return dve.tensor_scalar(out, in_, 1.0, None, ALU.mult)

        def heads_of(ap):
            return ap.rearrange("p (h c) -> p h c", h=heads)

        def read_a(n, par):
            if local or not is_sample(n):
                return
            dve.wait_ge(G["projA"], n + 1)
            if sample_is(n, 0):
                before(dve, "kT_bank", NS)
            wait(dve, G["kT_bank"], n - 1)
            if cross:
                dve.tensor_tensor(m.qkb[par][:, 0, 0:D], PJ0[:, 0:D], m.b_cross[:, 0, :], ALU.add).then_inc(G["evacA"], 1)
            else:
                dve.tensor_copy(m.qkb[par][:, :, 0:D], PJ0[:].rearrange("p (w c) -> p w c", w=2)).then_inc(G["evacA"], 1)

        def read_b(n, par):
            if not is_sample(n):
                return
            dve.wait_ge(G["projB"], n + 1)
            if cross:
                dve.tensor_tensor(m.qkb[par][:, 1, 0:D], PJ1[:, 0:D], m.b_cross[:, 1, :], ALU.add).then_inc(G["qk_ready"], 1)
                dve.tensor_tensor(m.V[:, n, 0:D], PJ1[:, D:2 * D], m.b_cross[:, 2, :], ALU.add).then_inc(G["evacB"], 1)
            else:
                copy(m.V[:, n, 0:D], PJ1[:, 0:D]).then_inc(G["evacB"], 1)

        def rotate(n, which):
            if not is_sample(n):
                return
            dve.wait_ge(G["evacB"] if which else G["evacA"], n + 1)
            wait(dve, G["rotsum"], n)

            def factor(kind, lo, hi):
                return m.rots[:, which, kind, lo:hi].unsqueeze(1).broadcast_to([P, heads, hi - lo])

            x, ra, rb = (heads_of(ap[:, which, :]) for ap in (m.raw, m.ra, m.rb))
            dve.tensor_tensor(ra, x, factor(0, 0, dh), ALU.mult).then_inc(G["rotated"], 1)
            for lo, hi in ((0, dh // 2), (dh // 2, dh)):
                dve.tensor_tensor(rb[:, :, lo:hi], x[:, :, dh // 2 - lo:dh - lo],
                                  factor(1, lo, hi), ALU.mult).then_inc(G["rotated"], 1)

        def norms(n, par):
            if not local or not is_sample(n):
                return [lambda: None] * 4
            ss, rn, rt = m.ss[par], m.rn[par], m.rt[par]

            def squares():
                wait(dve, G["qk_ready"], n - 1)
                dve.wait_ge(G["squared"], 2 * n + 2)
                dve.tensor_reduce(ss[:], m.sq[:].rearrange("p w (h c) -> p (w h) c", h=heads), AX.X,
                                  ALU.add).then_inc(G["sumsq"], 1)

            def clip():
                dve.wait_ge(G["sumsq"], n + 1)
                dve.tensor_scalar(ss[:], ss[:], NORM_FLOOR, 0.5, ALU.max, ALU.mult).then_inc(G["clipped"], 1)

            def halve():
                dve.wait_ge(G["clipped"], n + 1)
                dve.tensor_scalar(rt[:].bitcast(I32), ss[:].bitcast(I32), 1, None,
                                  ALU.logical_shift_right).then_inc(G["halved"], 1)

            def seed():
                dve.wait_ge(G["halved"], n + 1)
                dve.tensor_scalar(rn[:].bitcast(I32), rt[:].bitcast(I32), -1.0, RSQRT_MAGIC_OF_HALF,
                                  ALU.mult, ALU.add).then_inc(G["seeded"], 1)

            return squares, clip, halve, seed

        def quad_max(s, q):
            if not is_sample(s):
                return
            i = s * NQ + q
            dve.wait_ge(G["quad_scores"], i + 1)
            wait(dve, G["quad_probs"], i - 1)
            if sample_is(s * NQ + q, 0):
                before(dve, "quad_probs", ALL_QUADS)
            src = S[q % 2][:].rearrange("p (h c) -> p h c", h=QUAD)
            if causal:
                dve.tensor_tensor(m.masked[q % 2][:], src, m.mask[:].unsqueeze(1).broadcast_to([P, QUAD, P]),
                                  ALU.add).then_inc(G["quad_masked"], 1)
                dve.wait_ge(G["quad_masked"], i + 1)
                src = m.masked[q % 2][:]
            dve.tensor_reduce(m.negmax[q % 2][:], src, AX.X, ALU.max, negate=True).then_inc(G["quad_negmax"], 1)

        def normalise(n, par):
            if not is_sample(n):
                return
            dve.wait_ge(G["quad_out"], (n + 1) * NQ)
            wait(dve, G["o_ready"], n)
            if sample_is(n, 0):
                before(dve, "o_ready", NS)
                before(dve, "oT_bank", NS)
            dve.reciprocal(m.rec[:, 0:heads], m.rsum[par][:, 0:heads]).then_inc(G["rec_ready"], 1)
            dve.wait_ge(G["rec_ready"], n + 1)
            wait(dve, G["oT_bank"], n)
            dve.tensor_tensor(m.ob[:, 0:width].rearrange("p (h c) -> p h c", h=heads),
                              heads_of(OB[:, 0:width]),
                              m.rec[:, 0:heads].unsqueeze(2).broadcast_to([P, heads, dh]),
                              ALU.mult).then_inc(G["o_ready"], 1)

        def statistics(n, pieces, kept, source):
            wait(dve, G["mv_kept"], n)
            for i, piece in enumerate(pieces):
                dve.bn_stats(m.bn[:, i, :], piece).then_inc(G["stats"], 1)
            dve.wait_ge(G["stats"], len(pieces) * (n + 1))
            copy(kept, source).then_inc(G["kept"], 1)
            dve.bn_aggr(m.mv1[:], m.bn[:, 0:len(pieces), :].rearrange("p a b -> p (a b)")).then_inc(G["aggregated"], 1)
            dve.wait_ge(G["aggregated"], n + 1)
            copy(m.mv[:, n, :], m.mv1[:]).then_inc(G["mv_kept"], 1)

        def add_back(n, par):
            if not is_sample(n):
                return
            dve.wait_ge(G["wo_bank"], n + 1)
            if sample_is(n, 0):
                before(dve, "mv_kept", NS)
            R = m.Y if local else m.X
            row = m.row[par]
            if local:
                wait(dve, G["shifted"], n - 1)
            else:
                wait(dve, G["mv_kept"], n)
            dve.tensor_tensor(row[:], WB[:, 0:D], R[:, n, :], ALU.add).then_inc(G["added"], 1)
            dve.wait_ge(G["added"], n + 1)
            if local:
                copy(R[:, n, :], row[:]).then_inc(G["y_kept"], 1)
                return
            if cross:
                dve.tensor_tensor(row[:], row[:], m.b_cross[:, 3, :], ALU.add).then_inc(G["biased"], 1)
                dve.wait_ge(G["biased"], n + 1)
            statistics(n, (row[:],), R[:, n, :], row[:])

        def shifted_stats(n, par):
            if not local or not is_sample(n):
                return
            dve.wait_ge(G["shifted"], n + 1)
            statistics(n, (m.row[par][:, 0:P], TR1[:, 0:P]), m.YS[:, n, :], TR1[:, 0:P])

        def first_stats(lo, hi):
            for even in range(lo, hi, 2):
                wait(dve, G["first"], 2 * even)
                for n in (even, even + 1):
                    if n == 2 or n % 4 == 0:
                        dve.wait_ge(m.ld_x[4 if n == 2 else n // 4], 16)
                    dve.bn_stats(m.bn[:, n % 2, :], m.X[:, n, :]).then_inc(G["first"], 1)
                for n in (even, even + 1):
                    dve.wait_ge(G["first"], 2 * even + 1 + n % 2)
                    dve.bn_aggr(m.mv[:, n, :], m.bn[:, n % 2, :]).then_inc(G["first"], 1)
            dve.wait_ge(G["first"], 2 * hi)

        starts = 0

        def inverse_deviations(lo, hi):
            nonlocal starts
            wait(dve, G["start"], starts)
            dve.tensor_scalar(m.vare[:, lo:hi], m.mv[:, lo:hi, 1], EPS, None, ALU.add).then_inc(G["start"], 1)
            dve.wait_ge(G["start"], starts + 1)
            rsqrt(dve, m.rstd[:, lo:hi], m.vare[:, lo:hi], m.nt[:, lo:hi], G["start"], starts + 1)
            starts += 1 + RSQRT_OPS
            dve.wait_ge(G["start"], starts)

        def start():
            if kind == "self":
                first_stats(0, 2)
                inverse_deviations(0, 2)
                for n in range(2):
                    normed(n, n)
                return
            before(dve, "xT_bank", NS)
            if cross:
                dve.wait_ge(m.ld_cross, m.n_loads[m.ld_cross.name])
            if local:
                if not layer:
                    dve.wait_ge(m.ld_small, m.n_loads[m.ld_small.name])
                for w in range(2):
                    sc = m.qks[:, layer, w, :]
                    dve.tensor_tensor(m.rots[:, w, 0, :], m.rot[:, w, 0, :], sc, ALU.mult).then_inc(G["scaled"], 1)
                    for t in range(2):
                        lo, hi = t * dh // 2, (t + 1) * dh // 2
                        other = sc[:, (1 - t) * dh // 2:(2 - t) * dh // 2]
                        dve.tensor_tensor(m.rots[:, w, 1, lo:hi], m.rot[:, w, 1, lo:hi], other,
                                          ALU.mult).then_inc(G["scaled"], 1)
                dve.wait_ge(G["scaled"], 6)
            if ph.prev:
                for n in range(2):
                    normed(n, n)

        def more_statistics(s, q):
            if kind == "self" and s == -2 and q == 1:
                first_stats(2, 6)
            if kind == "self" and s == -2 and q == 3:
                first_stats(6, 10)
            if kind == "self" and s == -1 and q == 1:
                first_stats(10, 14)
            if kind == "self" and s == -1 and q == 3:
                first_stats(14, NS)
                inverse_deviations(2, NS)
            if q != (2 if cross and s < 0 else 1):
                return
            if ph.prev and not (local and layer):
                for first_body, (lo, hi) in ((-2, (2, NS - 3)), (2, (NS - 3, NS))):
                    if sample_is(s, first_body):
                        before(dve, "mv_kept", hi)
                        inverse_deviations(lo, hi)
            if ph.next and sample_is(s, NS - 2 if local else 3):
                dve.wait_ge(G["mv_kept"], 2)
                inverse_deviations(0, 2)

        def read_kT(n, par, part):
            if not is_sample(n):
                return
            dve.wait_ge(G["kT_bank"], n + 1)
            if kind == "self" and sample_is(n, 0):
                dve.wait_ge(m.ld_const, m.n_loads[m.ld_const.name])
            wait(dve, G["quad_scores"], (n - 1) * NQ)
            if isinstance(n, int) and n <= 1:
                before(dve, "quad_scores", ALL_QUADS - QUADS_BEFORE * (1 - n))
            if local:
                if not layer and isinstance(n, int) and n <= 1:
                    dve.wait_ge(G["cleared"], 2 * n + 2)
                lo, hi = part * dh, (part + 1) * dh
                dve.tensor_copy(key_blocks(par)[lo:hi, :, part * P:(part + 1) * P],
                                TR1[lo:hi, :].rearrange("p (t c) -> p t c", t=4)).then_inc(G["kT_ready"], 1)
            else:
                dve.tensor_tensor(m.kB[par][:, part, :].rearrange("p (h c) -> p h c", h=8),
                                  TR1[:, part * P:(part + 1) * P].unsqueeze(1).broadcast_to([P, 8, P]),
                                  m.own[:].unsqueeze(2).broadcast_to([P, 8, P]), ALU.mult).then_inc(G["kT_ready"], 1)

        def slot(s, par, q, inputs_done=False):
            nxt = s + AHEAD
            if q == 0:
                if not ((ph.prev or kind == "self") and isinstance(nxt, int) and nxt <= 1):
                    normed(nxt, par)
                elif nxt >= 0:
                    keep_normed(nxt)
            if isinstance(s, int):
                more_statistics(s, q)
            if q == 0 and local:
                normalise(s - 2, par)
            if q == 1 and local:
                rotate(nxt, 0)
                rotate(nxt, 1)
                squares, clip, halve, seed = norms(nxt, par)
                squares()
            if q == 2:
                normalise(s - 1, 1 - par)
            quad_max(s, q)
            if q < 2 and not local:
                read_kT(s + 1, 1 - par, q)
            if local and q == 0:
                shifted_stats(s - 3, 1 - par)
                if not (isinstance(nxt, int) and nxt <= 1):
                    keep_normed(nxt)
            elif local:
                clip()
                halve()
                read_kT(s + 1, 1 - par, 0)
                seed()
                read_kT(s + 1, 1 - par, 1)
                add_back(s - 2, par)
            elif q == 2:
                read_a(nxt, par)
            elif q == 3:
                read_b(nxt, par)
                add_back(s - 1, 1 - par)

        return start, slot, NQ, nothing

    def scalar(act):
        def read_xT(n, par):
            if not is_sample(n):
                return
            act.wait_ge(G["xT_bank"], n + 1)
            if sample_is(n, 0):
                before(act, "projB", NS)
            wait(act, G["projC"] if local else G["projB"], n - 1)
            src = TR0[:, 0:nT * P].rearrange("p (t c) -> p t c", t=nT)
            if not local:
                act.copy(m.xT[par][:, 0:nT, :], src).then_inc(G["xT_ready"], 1)
                return
            act.copy(m.xT[par][:, 1, 1:P], src[:, 1, 0:P - 1]).then_inc(G["xT_ready"], 1)
            act.copy(m.xT[par][:, 0, :], src[:, 0, :]).then_inc(G["xT_ready"], 1)

        def read_qT(n, par):
            if not is_sample(n):
                return
            act.wait_ge(G["qT_bank"], n + 1)
            wait(act, G["quad_scores"], (n - 1) * NQ)
            if isinstance(n, int) and n <= 1:
                before(act, "quad_scores", ALL_QUADS - QUADS_BEFORE * (1 - n))
            act.activation(m.qT[par][:, 0:OT_TILES, :],
                           TR0[:, 0:width].rearrange("p (t c) -> p t c", t=OT_TILES), ACT.Copy,
                           scale=1.0 if local else 0.25).then_inc(G["qT_ready"], 1)

        def square(n, which):
            if not is_sample(n):
                return
            act.wait_ge(G["projB"] if which else G["projA"], n + 1)
            wait(act, G["rotated"], ROT * n)
            wait(act, G["sumsq"], n)
            done = G["evacB"] if which else G["evacA"]
            act.copy(m.raw[:, which, :], (PJ1 if which else PJ0)[:]).then_inc(done, 1)
            act.wait_ge(done, n + 1)
            act.activation(m.sq[:, which, :], m.raw[:, which, :], ACT.Square).then_inc(G["squared"], 1)

        def read_c(n):
            if not is_sample(n):
                return
            act.wait_ge(G["projC"], n + 1)
            act.copy(m.V[:, n, :], PJ0[:]).then_inc(G["evacC"], 1)

        def read_pT(s, q):
            if not is_sample(s):
                return
            i = s * NQ + q
            act.wait_ge(G["quad_pT_bank"], i + 1)
            wait(act, G["quad_out"], i - 1)
            if isinstance(i, int) and i <= 1:
                before(act, "quad_out", ALL_QUADS - 1 + i)
            act.copy(m.pT[q % 2][:], PTB[:].rearrange("p (h c) -> p h c", h=QUAD)).then_inc(G["quad_pT"], 1)

        def exponentials(s, par, q):
            if not is_sample(s):
                return
            i = s * NQ + q
            act.wait_ge(G["quad_negmax"], i + 1)
            wait(act, G["quad_pT_bank"], i - 1)
            if isinstance(i, int) and i <= 1:
                before(act, "quad_pT_bank", ALL_QUADS - 1 + i)
            if q == 0 and isinstance(s, int) and s <= 1:
                before(act, "rec_ready", NS - 1 + s)
            if q == 0:
                wait(act, G["rec_ready"], s - 1)
            src = m.masked[q % 2] if causal else S[q % 2][:].rearrange("p (h c) -> p h c", h=QUAD)
            for j in range(QUAD):
                h = QUAD * q + j
                last = act.activation(m.probs[q % 2][:, j, :], src[:, j, :], ACT.Exp,
                                      bias=m.negmax[q % 2][:, j:j + 1],
                                      accum_out=m.rsum[par][:, h:h + 1])
            last.then_inc(G["quad_probs"], 1)

        def read_oT(n):
            if not is_sample(n):
                return
            act.wait_ge(G["oT_bank"], n + 1)
            wait(act, G["wo_bank"], n)
            if sample_is(n, 0):
                before(act, "wo_bank", NS)
            act.copy(m.oT[:, 0:OT_TILES, :],
                     TR1[:, 0:width].rearrange("p (t c) -> p t c", t=OT_TILES)).then_inc(G["oT_ready"], 1)

        def start():
            if not local:
                return
            before(act, "projB", NS)
            for i in range(2):
                act.memzero(m.xT[i][:, 1, 0:1]).then_inc(G["zeroed"], 1)
            act.wait_ge(G["zeroed"], 2)

        def slot(s, par, q, inputs_done=False):
            nxt = s + AHEAD
            if local and q == 0 and not inputs_done:
                read_xT(nxt, par)
            read_pT(*((s, q - LAG) if q >= LAG else (s - 1, NQ + q - LAG)))
            if not local and q == 0:
                read_qT(s + 1, 1 - par)
                read_xT(nxt, par)
            if local and q == 0:
                square(nxt, 0)
            elif local:
                read_c(nxt)
                read_qT(s + 1, 1 - par)
            if local and q == 0 and inputs_done:
                square(nxt, 1)
            exponentials(s, par, q)
            if local and q == 0:
                if not inputs_done:
                    square(nxt, 1)
                read_oT(s - 2)
            elif q == 2 and not local:
                read_oT(s - 1)

        return start, slot, NQ, read_xT

    def gpsimd(pool):
        if not local:
            return

        def finish(n, par):
            if not is_sample(n):
                return
            qk = m.qkb[par][:]
            ss, y, t = m.ss[par][:], m.rn[par][:], m.rt[par][:]
            wait(pool, G["kT_bank"], n - 1)
            if sample_is(n, 0):
                before(pool, "kT_bank", NS)
            pool.wait_ge(G["rotated"], ROT * (n + 1))
            pool.tensor_tensor(qk, m.ra, m.rb, ALU.add).then_inc(G["rotsum"], 1)
            pool.wait_ge(G["seeded"], n + 1)
            step = n * 4 * NEWTON
            for i in range(NEWTON):
                if i:
                    pool.wait_ge(G["newton"], step + 4 * i)
                pool.tensor_tensor(t, y, y, ALU.mult).then_inc(G["newton"], 1)
                pool.wait_ge(G["newton"], step + 4 * i + 1)
                pool.tensor_tensor(t, t, ss, ALU.mult).then_inc(G["newton"], 1)
                pool.wait_ge(G["newton"], step + 4 * i + 2)
                pool.tensor_tensor(t, m.three_halves[:], t, ALU.subtract).then_inc(G["newton"], 1)
                pool.wait_ge(G["newton"], step + 4 * i + 3)
                pool.tensor_tensor(y, y, t, ALU.mult).then_inc(G["newton"], 1)
            pool.wait_ge(G["newton"], step + 4 * NEWTON)
            pool.wait_ge(G["rotsum"], n + 1)
            split = qk.rearrange("p w (h c) -> p (w h) c", h=heads)
            pool.tensor_tensor(split, split, y.unsqueeze(2).broadcast_to([P, 2 * heads, dh]),
                               ALU.mult).then_inc(G["qk_ready"], 1)

        def clear():
            pool.wait_ge(G["qk_ready"], 1)
            for i in range(2):
                before(pool, "quad_scores", ALL_QUADS - QUADS_BEFORE * (1 - i))
                for part in range(2):
                    lo = (1 - part) * dh
                    wait(pool, G["cleared"], 2 * i + part)
                    pool.memset(key_blocks(i)[lo:lo + dh, :, part * P:(part + 1) * P], 0.0).then_inc(G["cleared"], 1)

        if not layer:
            pool.memset(m.three_halves[:], 1.5).then_inc(G["constant"], 1)
            pool.wait_ge(G["constant"], 1)
        finish(0, 0)
        if not layer:
            clear()
            pool.wait_ge(G["cleared"], 4)
        finish(1, 1)
        with pool.Fori(1, NS // 2) as pair:
            finish(pair * 2, 0)
            finish(pair * 2 + 1, 1)

    ph.sync, ph.tensor, ph.vector, ph.scalar, ph.gpsimd = sync, tensor, vector, scalar, gpsimd
    return ph


def mlp(nc, m, layer, out):
    NG = NS // GS
    N = GS * P
    final = layer == DEPTH - 1
    tag = f"mlp{layer}_"
    G = {n: nc.alloc_semaphore(name=tag + n) for n in (
        "start", "hn_ready", "hT_bank", "hT_ready", "tile_in", "gate_ready", "hid_ready", "out_bank",
        "biased", "added", "stored")}
    NORMS = 2 * GS
    A, GB, W2B, TB = m.banks[0:2], m.banks[2:4], m.banks[4:6], m.banks[6]

    ph = Phase()
    ph.G, ph.prev, ph.next = G, None, None
    QUADS = NS * HEADS // QUAD

    ph.frees = {"oT_ready": [("hid_ready", NG * FT)],
                "quad_probs": [("added", NS), ("tile_in", NG * FT), ("hT_bank", NG)],
                "quad_pT": [("hT_ready", KT * NG)], "quad_out": [("out_bank", NG)],
                "quad_pT_bank": [("hid_ready", NG * FT), ("out_bank", NG)],
                "xT_bank": [("added", GS)],
                "w_mlp": [("tile_in", NG * FT), ("out_bank", NG)]}

    def is_group(i):
        return not isinstance(i, int) or i < NG

    def before(eng, name, count):
        if ph.prev:
            eng.wait_ge(ph.prev.G[name], count)

    def tensor(pe):
        def transposes(i):
            if not is_group(i):
                return
            pe.wait_ge(G["hn_ready"], NORMS * (i + 1))
            wait(pe, G["hT_ready"], KT * i)
            for gs in range(GS):
                for k in range(KT):
                    at = (gs * KT + k) * P
                    last = pe.transpose(TB[:, at:at + P], m.hn[:, gs, k * P:(k + 1) * P], m.ident[:])
            last.then_inc(G["hT_bank"], 1)

        def lending(i):
            return ph.next and isinstance(i, int) and i >= NG - 2

        def lead():
            before(pe, "quad_pT", QUADS)
            transposes(0)

        def between():
            pe.wait_ge(m.ld_mlp, 3 * 16 * (layer + 1))
            before(pe, "qT_ready", NS)
            before(pe, "evacC", NS)
            tile(0, 0)

        def ready():
            for name, count in (("kept", NS), ("added", NS), ("quad_masked", QUADS)):
                before(pe, name, count)

        def tile(i, f):
            lo, nf = TILES[f]
            if f == 0:
                pe.wait_ge(G["hT_ready"], KT * (i + 1))
            wait(pe, G["hid_ready"], i * FT + f - 1)
            if lending(i) and f < 2:
                n = i - (NG - 2) + 1
                if f == 0:
                    pe.wait_ge(ph.next.G["xT_ready"], ph.next.XR * n)
                pe.wait_ge(ph.next.G["evacB" if f else "evacA"], n)
            for bank, at, rows in (((GB[f % 2], FULL + lo, P), (A[f % 2], lo, P)) if nf == P else
                                   ((GB[f % 2], 2 * FULL, MIXED),)):
                for k in range(KT):
                    last = pe.matmul(bank[0:rows, 0:N], m.w_1[:, k, at:at + rows], m.hT[:, k, :],
                                     start=k == 0, stop=k == KT - 1)
            last.then_inc(G["tile_in"], 1)

        def first(i):
            for f in range(1 if isinstance(i, int) and i == 0 else 0, FT):
                tile(i, f)
            transposes(i + 1)
            if lending(i):
                pe.wait_ge(G["hid_ready"], i * FT + FT - 1)

        def second(i):
            wait(pe, G["added"], GS * i)
            for f, (lo, nf) in enumerate(TILES):
                pe.wait_ge(G["hid_ready"], i * FT + f + 1)
                for gs in range(GS):
                    last = pe.matmul(W2B[gs][:, 0:D], m.hid[f][0:nf, gs * P:(gs + 1) * P],
                                     m.w_2[0:nf, f, :], start=f == 0, stop=f == FT - 1)
            last.then_inc(G["out_bank"], 1)

        return nothing, lead, between, ready, first, second, nothing

    def scalar(act):
        def first(i):
            for f, (lo, nf) in enumerate(TILES):
                act.wait_ge(G["tile_in"], i * FT + f + 1)
                wait(act, G["hid_ready"], i * FT + f - 1)
                g = 0 if nf == P else GATES_AT
                act.activation(m.gate[f % 2][0:nf, :], GB[f % 2][g:g + nf, 0:N], ACT.Gelu,
                               bias=m.b_1[g:g + nf, layer, 1, f:f + 1]).then_inc(G["gate_ready"], 1)

        def ready():
            before(act, "quad_pT_bank", QUADS)

        return nothing, nothing, nothing, ready, first, nothing, nothing

    def vector(dve):
        def normed(i):
            if not is_group(i):
                return
            wait(dve, G["hT_bank"], i)
            for gs in range(GS):
                for k, src in enumerate((m.Y, m.YS)):
                    s = i * GS + gs
                    dve.tensor_scalar(m.hn[:, gs, k * P:(k + 1) * P], src[:, s, 0:P], m.mv[:, s, 0:1],
                                      m.rstd[:, bass.ds(s, 1)], ALU.subtract, ALU.mult).then_inc(G["hn_ready"], 1)

        def read_hT(i):
            if not is_group(i):
                return
            dve.wait_ge(G["hT_bank"], i + 1)
            wait(dve, G["tile_in"], FT * i)
            for k in range(KT):
                dve.tensor_scalar(m.hT[:, k, :].rearrange("p (g c) -> p g c", g=GS),
                                  TB[:].rearrange("p (g k c) -> p k g c", g=GS, k=KT)[:, k],
                                  m.ln_g[:, layer, k:k + 1], m.ln_b[:, layer, k:k + 1],
                                  ALU.mult, ALU.add).then_inc(G["hT_ready"], 1)

        def inverse_deviations(lo, hi, count):
            dve.tensor_scalar(m.vare[:, lo:hi], m.mv[:, lo:hi, 1], EPS, None, ALU.add).then_inc(G["start"], 1)
            dve.wait_ge(G["start"], count + 1)
            rsqrt(dve, m.rstd[:, lo:hi], m.vare[:, lo:hi], m.nt[:, lo:hi], G["start"], count + 1)
            dve.wait_ge(G["start"], count + 1 + RSQRT_OPS)

        EARLY = NS - 3

        def early():
            before(dve, "mv_kept", EARLY)
            if not ph.prev:
                inverse_deviations(0, GS, 0)
            before(dve, "kept", EARLY)
            before(dve, "y_kept", EARLY)
            before(dve, "quad_probs", QUADS)
            normed(0)

        def lead():
            read_hT(0)

        def between():
            inverse_deviations(GS, EARLY, RSQRT_OPS + 1 if not ph.prev else 0)

        def ready():
            normed(1)
            for name in ("quad_pT_bank", "quad_out"):
                before(dve, name, QUADS)

        def late():
            for name in ("mv_kept", "kept", "y_kept"):
                before(dve, name, NS)
            inverse_deviations(EARLY, NS, (1 + RSQRT_OPS) * (1 if ph.prev else 2))

        def first(i):
            for f, (lo, nf) in enumerate(TILES):
                dve.wait_ge(G["gate_ready"], i * FT + f + 1)
                wait(dve, G["out_bank"], i)
                dve.scalar_tensor_tensor(m.hid[f][0:nf, :], (A if nf == P else GB)[f % 2][0:nf, 0:N], m.b_1[0:nf, layer, 0, f:f + 1],
                                         m.gate[f % 2][0:nf, :], ALU.add, ALU.mult).then_inc(G["hid_ready"], 1)
            read_hT(i + 1)
            normed(i + 2)

        def second(i):
            dve.wait_ge(G["out_bank"], i + 1)
            dve.wait_ge(G["biased"], (1 + final) * (i + 1))
            for gs in range(GS):
                s = i * GS + gs
                dve.tensor_tensor(m.Y[:, s, :], W2B[gs][:, 0:D], m.Y[:, s, :], ALU.add).then_inc(G["added"], 1)

        return early, lead, between, ready, first, second, late

    def gpsimd(pool):
        def body(i):
            pool.wait_ge(G["hn_ready"], NORMS * (i + 1))
            y = m.Y[:, bass.ds(i * GS, GS), :]
            pool.tensor_tensor(y, y, m.b_2[:, layer, :].unsqueeze(1).broadcast_to([P, GS, D]),
                               ALU.add).then_inc(G["biased"], 1)
            if final:
                pool.wait_ge(G["biased"], 2 * i + 1)
                pool.tensor_tensor(y, y, m.X[:, bass.ds(i * GS, GS), :], ALU.add).then_inc(G["biased"], 1)

        with pool.Fori(0, NG, 1) as i:
            body(i)

    def sync(sp):
        if not final:
            return
        with sp.Fori(0, NG, 1) as i:
            sp.wait_ge(G["added"], GS * (i + 1))
            sp.dma_start(out.rearrange("s t d -> t s d")[:, bass.ds(i * GS, GS), :],
                         m.Y[:, bass.ds(i * GS, GS), :]).then_inc(G["stored"], 16)
        sp.wait_ge(G["stored"], 16 * NG)

    ph.sync, ph.tensor, ph.vector, ph.scalar, ph.gpsimd = sync, tensor, vector, scalar, gpsimd
    return ph


def shape_constants():
    f = np.float32
    half = np.arange(0, DH, 2, dtype=f)
    inv_freq = (f(1.0) / f(10000.0) ** (half / f(DH))).astype(f)
    t = np.arange(P, dtype=f)
    freqs = t[:, None] * inv_freq[None, :]
    freqs = np.concatenate([freqs, freqs], -1)
    base = (half + f(0.4 * DH)) / f(1.4 * DH)
    power = (t - P // 2) / f(P // 2)
    scale = base[None, :] ** power[:, None]
    scale = np.concatenate([scale, scale], -1)
    sign = np.concatenate([-np.ones(DH // 2, f), np.ones(DH // 2, f)])[None, :]
    cos, sin = np.cos(freqs), np.sin(freqs) * sign
    rot = np.stack([np.stack([8.0 * cos * scale, 8.0 * sin * scale], 1),
                    np.stack([cos / scale, sin / scale], 1)], 1).astype(f)
    q, k = np.arange(P)[:, None], np.arange(P)[None, :]
    return {"c_ident": np.eye(P, dtype=f), "c_shift": (k == q + 1).astype(f),
            "c_mask": np.where(k <= q, 0.0, MASKED).astype(f), "c_rot": rot,
            "c_own": (q // 16 == np.arange(8)[None, :]).astype(f)}


def kernel(**inputs):
    import concourse.bacc as _bacc
    from concourse.bass_utils import run_bass_kernel_spmd as _run

    g = {k: np.asarray(v) for k, v in inputs.items()}

    def tiles(w):
        return w.reshape(-1, P, w.shape[-1]).transpose(1, 0, 2)

    def biases(b):
        out = np.zeros((DEPTH, 2, FT, P), b.dtype)
        b = b.reshape(DEPTH, 2, HID)
        out[:, :, 0:FT - 1] = b[:, :, 0:FULL].reshape(DEPTH, 2, FT - 1, P)
        out[:, 0, FT - 1, 0:REST] = b[:, 0, FULL:]
        out[:, 1, FT - 1, GATES_AT:MIXED] = b[:, 1, FULL:]
        return out.transpose(3, 0, 1, 2)

    arrays = {
        "x": g["x"], "ctx": g["ctx_1024"],
        "w_self": tiles(np.concatenate([g[f"L0_attn_W{c}"].reshape(D, D).T for c in "QKV"], 1)),
        "wo_self": tiles(g["L0_attn_WO"].transpose(0, 2, 1).reshape(D, D)),
        "w_cross": tiles(np.concatenate([g[f"L0_xattn_W_{c}"].T for c in "qkv"], 1)),
        "wo_cross": tiles(g["L0_xattn_W_o"].T),
        **{f"b_{c}": g[f"L0_xattn_b_{c}"].reshape(1, D) for c in "qkvo"},
        "w_qkv": np.stack([tiles(w) for w in g["L0_ffn_wqkv"]]),
        "wo_loc": np.stack([tiles(w) for w in g["L0_ffn_wo"]]),
        "w_1": np.stack([tiles(np.concatenate([w[:, 0:FULL], w[:, HID:HID + FULL], w[:, FULL:HID],
                                               np.zeros((D, GATES_AT - REST), w.dtype), w[:, HID + FULL:]], 1))
                         for w in g["L0_ffn_w1"]]),
        "w_2": g["L0_ffn_w2"],
        "b1": biases(g["L0_ffn_b1"]), "b2": g["L0_ffn_b2"],
        "ln_g": g["L0_ffn_ln_g"].reshape(DEPTH, KT, P).transpose(2, 0, 1),
        "ln_b": g["L0_ffn_ln_b"].reshape(DEPTH, KT, P).transpose(2, 0, 1),
        "q_scale": g["L0_ffn_q_scale"], "k_scale": g["L0_ffn_k_scale"],
        **shape_constants(),
    }
    arrays = {f"in_{k}": np.ascontiguousarray(v) for k, v in arrays.items()}
    nc = _bacc.Bacc("TRN2", target_bir_lowering=False, num_devices=1)
    args = {k[3:]: nc.dram_tensor(k, v.shape, mybir.dt.from_np(v.dtype), kind="ExternalInput").ap()
            for k, v in arrays.items()}
    out = nc.dram_tensor("out_0", (NS, P, D), F32, kind="ExternalOutput").ap()
    decoder_kernel(nc, args, out)
    r = _run(nc, [arrays], core_ids=[0])
    return r.results[0]["out_0"]
```
